# Optimizing a Trainium2 kernel written in Bass

```python
import numpy as np
import jax
import jax.numpy as jnp

def _softmax(x, axis=-1):
    return jax.nn.softmax(x, axis=axis)

def _gelu(x):
    return jax.nn.gelu(x, approximate=True)

def _silu(x):
    return jax.nn.silu(x)

def _sigmoid(x):
    return jax.nn.sigmoid(x)

def _layernorm(x, axis=-1, eps=1e-05):
    m = jnp.mean(x, axis=axis, keepdims=True)
    v = jnp.var(x, axis=axis, keepdims=True)
    return (x - m) / jnp.sqrt(v + eps)

def _scatter_add(tgt, idx, src, axis=0):
    return tgt.at[idx].add(src)

def _segment_sum(src, seg, n):
    return jax.ops.segment_sum(src, seg, n)
kernel_name = 'mk_recurrent_d2_jaxref_r8_3e0e69'

def setup_inputs(seed: int=0):
    np.random.seed(seed)
    _w = jnp.asarray

    def _L0_attn_setup():
        import jax, jax.numpy as jnp
        import numpy as np
        BASE_THETA = 0.5
        K_DOP = 0.2
        K_NOR = 0.15
        K_SERO = 0.1
        DIM = 128
        key = jax.random.key(seed)
        ks = jax.random.split(key, 9)
        scale = 1.0 / np.sqrt(DIM)
        x = jax.random.normal(ks[0], (2, 256, DIM), dtype=jnp.float32)
        Wq = jax.random.normal(ks[1], (DIM, DIM), dtype=jnp.float32) * scale
        bq = jnp.zeros((DIM,), dtype=jnp.float32)
        Wk = jax.random.normal(ks[2], (DIM, DIM), dtype=jnp.float32) * scale
        bk = jnp.zeros((DIM,), dtype=jnp.float32)
        Wv = jax.random.normal(ks[3], (DIM, DIM), dtype=jnp.float32) * scale
        bv = jnp.zeros((DIM,), dtype=jnp.float32)
        Wo = jax.random.normal(ks[4], (DIM, DIM), dtype=jnp.float32) * scale
        bo = jnp.zeros((DIM,), dtype=jnp.float32)
        return {'x': x, 'Wq': Wq, 'bq': bq, 'Wk': Wk, 'bk': bk, 'Wv': Wv, 'bv': bv, 'Wo': Wo, 'bo': bo}
    _L0_attn_in = _L0_attn_setup()

    def _L0_ffn_setup():
        import jax, jax.numpy as jnp
        import numpy as np
        H = 128
        I = 256
        E = 8
        B, S = (2, 512)
        EPS = 1e-05
        INIT = 0.02

        def _layernorm(x, w, b):
            mu = jnp.mean(x, axis=-1, keepdims=True)
            var = jnp.mean(jnp.square(x - mu), axis=-1, keepdims=True)
            return (x - mu) * jax.lax.rsqrt(var + EPS) * w + b
        key = jax.random.key(seed)
        ks = jax.random.split(key, 9)
        return {'hidden_states': jax.random.normal(ks[0], (B, S, H), jnp.float32), 'ln_w': jnp.ones((H,), jnp.float32), 'ln_b': jnp.zeros((H,), jnp.float32), 'router_w': jax.random.normal(ks[1], (H, E), jnp.float32) * INIT, 'gate_w': jax.random.normal(ks[2], (E, H, I), jnp.float32) * INIT, 'up_w': jax.random.normal(ks[3], (E, H, I), jnp.float32) * INIT, 'down_w': jax.random.normal(ks[4], (E, I, H), jnp.float32) * INIT, 'sh_gate': jax.random.normal(ks[5], (H, I), jnp.float32) * INIT, 'sh_up': jax.random.normal(ks[6], (H, I), jnp.float32) * INIT, 'sh_down': jax.random.normal(ks[7], (I, H), jnp.float32) * INIT}
    _L0_ffn_in = _L0_ffn_setup()

    def _L1_attn_setup():
        import jax, jax.numpy as jnp
        import numpy as np
        BATCH, L, D_MODEL = (2, 128, 128)
        D_STATE, D_CONV, EXPAND = (16, 4, 2)
        D_INNER = EXPAND * D_MODEL
        DT_RANK = max(1, -(-D_MODEL // 16))

        def _forward(x, W_in, conv_w, conv_b, W_x, W_dt, b_dt, A_log, D, W_out):
            xv = x @ W_in
            xc = jnp.transpose(xv, (0, 2, 1))
            xc = jax.lax.conv_general_dilated(xc, conv_w, window_strides=(1,), padding=[(D_CONV - 1, 0)], dimension_numbers=('NCH', 'OIH', 'NCH'), feature_group_count=D_INNER)
            xv = jnp.transpose(xc, (0, 2, 1)) + conv_b
            xv = jax.nn.silu(xv)
            ssm = xv @ W_x
            dt_raw = ssm[..., :DT_RANK]
            Bp = ssm[..., DT_RANK:DT_RANK + D_STATE]
            Cp = ssm[..., DT_RANK + D_STATE:]
            delta = jax.nn.softplus(dt_raw @ W_dt + b_dt)
            A = -jnp.exp(A_log)
            dA = jnp.exp(delta[..., None] * A)
            dBx = delta[..., None] * Bp[:, :, None, :] * xv[..., None]

            def comb(c1, c2):
                a1, b1 = c1
                a2, b2 = c2
                return (a1 * a2, a2 * b1 + b2)
            _, h = jax.lax.associative_scan(comb, (dA, dBx), axis=1)
            y = jnp.einsum('bldn,bln->bld', h, Cp)
            y = y + xv * D
            return y @ W_out
        key = jax.random.key(seed)
        ks = jax.random.split(key, 10)
        s = 0.02
        x = jax.random.normal(ks[0], (BATCH, L, D_MODEL), jnp.float32)
        W_in = jax.random.normal(ks[1], (D_MODEL, D_INNER), jnp.float32) * s
        conv_w = jax.random.normal(ks[2], (D_INNER, 1, D_CONV), jnp.float32) * s
        conv_b = jax.random.normal(ks[3], (D_INNER,), jnp.float32) * s
        W_x = jax.random.normal(ks[4], (D_INNER, DT_RANK + 2 * D_STATE), jnp.float32) * s
        W_dt = jax.random.normal(ks[5], (DT_RANK, D_INNER), jnp.float32) * s
        b_dt = jax.random.normal(ks[6], (D_INNER,), jnp.float32) * s
        A_log = jnp.log(jnp.broadcast_to(jnp.arange(1, D_STATE + 1, dtype=jnp.float32), (D_INNER, D_STATE)))
        D = jnp.ones((D_INNER,), jnp.float32)
        W_out = jax.random.normal(ks[7], (D_INNER, D_MODEL), jnp.float32) * s
        return {'x': x, 'W_in': W_in, 'conv_w': conv_w, 'conv_b': conv_b, 'W_x': W_x, 'W_dt': W_dt, 'b_dt': b_dt, 'A_log': A_log, 'D': D, 'W_out': W_out}
    _L1_attn_in = _L1_attn_setup()

    def _L1_ffn_setup():
        import jax, jax.numpy as jnp
        import numpy as np
        DIM = 128
        HIDDEN = 384
        SCALE = 1.0 / 127.0

        def _dequant(w_int, dtype):
            return w_int.astype(dtype) * jnp.asarray(SCALE, dtype)
        key = jax.random.key(seed)
        k_x, k_g, k_u, k_d = jax.random.split(key, 4)
        x = jax.random.normal(k_x, (4, 256, DIM), dtype=jnp.float32)
        w_gate = jax.random.randint(k_g, (HIDDEN, DIM), -127, 128, dtype=jnp.int32)
        w_up = jax.random.randint(k_u, (HIDDEN, DIM), -127, 128, dtype=jnp.int32)
        w_down = jax.random.randint(k_d, (DIM, HIDDEN), -127, 128, dtype=jnp.int32)
        return {'x': x, 'w_gate': w_gate, 'w_up': w_up, 'w_down': w_down}
    _L1_ffn_in = _L1_ffn_setup()
    _d = {'L0_attn_x': _L0_attn_in['x'], 'L0_attn_Wq': _L0_attn_in['Wq'], 'L0_attn_bq': _L0_attn_in['bq'], 'L0_attn_Wk': _L0_attn_in['Wk'], 'L0_attn_bk': _L0_attn_in['bk'], 'L0_attn_Wv': _L0_attn_in['Wv'], 'L0_attn_bv': _L0_attn_in['bv'], 'L0_attn_Wo': _L0_attn_in['Wo'], 'L0_attn_bo': _L0_attn_in['bo'], 'L0_ffn_ln_w': _L0_ffn_in['ln_w'], 'L0_ffn_ln_b': _L0_ffn_in['ln_b'], 'L0_ffn_router_w': _L0_ffn_in['router_w'], 'L0_ffn_gate_w': _L0_ffn_in['gate_w'], 'L0_ffn_up_w': _L0_ffn_in['up_w'], 'L0_ffn_down_w': _L0_ffn_in['down_w'], 'L0_ffn_sh_gate': _L0_ffn_in['sh_gate'], 'L0_ffn_sh_up': _L0_ffn_in['sh_up'], 'L0_ffn_sh_down': _L0_ffn_in['sh_down'], 'L1_attn_W_in': _L1_attn_in['W_in'], 'L1_attn_conv_w': _L1_attn_in['conv_w'], 'L1_attn_conv_b': _L1_attn_in['conv_b'], 'L1_attn_W_x': _L1_attn_in['W_x'], 'L1_attn_W_dt': _L1_attn_in['W_dt'], 'L1_attn_b_dt': _L1_attn_in['b_dt'], 'L1_attn_A_log': _L1_attn_in['A_log'], 'L1_attn_D': _L1_attn_in['D'], 'L1_attn_W_out': _L1_attn_in['W_out'], 'L1_ffn_w_gate': _L1_ffn_in['w_gate'], 'L1_ffn_w_up': _L1_ffn_in['w_up'], 'L1_ffn_w_down': _L1_ffn_in['w_down']}
    _x0 = _d['L0_attn_x']
    _d['L0_attn_x'] = jax.random.normal(jax.random.fold_in(jax.random.key(seed), 1), (8, 512, 128), dtype=_x0.dtype)
    del _x0
    return _d

def reference(L0_attn_x, L0_attn_Wq, L0_attn_bq, L0_attn_Wk, L0_attn_bk, L0_attn_Wv, L0_attn_bv, L0_attn_Wo, L0_attn_bo, L0_ffn_ln_w, L0_ffn_ln_b, L0_ffn_router_w, L0_ffn_gate_w, L0_ffn_up_w, L0_ffn_down_w, L0_ffn_sh_gate, L0_ffn_sh_up, L0_ffn_sh_down, L1_attn_W_in, L1_attn_conv_w, L1_attn_conv_b, L1_attn_W_x, L1_attn_W_dt, L1_attn_b_dt, L1_attn_A_log, L1_attn_D, L1_attn_W_out, L1_ffn_w_gate, L1_ffn_w_up, L1_ffn_w_down):

    def _L0_attn_ref(x, Wq, bq, Wk, bk, Wv, bv, Wo, bo):
        import jax, jax.numpy as jnp
        import numpy as np
        BASE_THETA = 0.5
        K_DOP = 0.2
        K_NOR = 0.15
        K_SERO = 0.1
        DIM = 128
        q = jnp.einsum('bsd,ed->bse', x, Wq) + bq
        k = jnp.einsum('bsd,ed->bse', x, Wk) + bk
        v = jnp.einsum('bsd,ed->bse', x, Wv) + bv
        qk = jnp.einsum('bsd,btd->bst', q, k)
        theta = BASE_THETA + K_DOP * jax.nn.sigmoid(qk) + K_NOR * jnp.tanh(qk) + K_SERO * jax.nn.relu(qk)
        attn = jax.nn.softmax(theta, axis=-1)
        out = jnp.einsum('bst,btd->bsd', attn, v)
        return jnp.einsum('bsd,ed->bse', out, Wo) + bo

    def _L0_ffn_ref(hidden_states, ln_w, ln_b, router_w, gate_w, up_w, down_w, sh_gate, sh_up, sh_down):
        import jax, jax.numpy as jnp
        import numpy as np
        H = 128
        I = 256
        E = 8
        B, S = (2, 512)
        EPS = 1e-05
        INIT = 0.02

        def _layernorm(x, w, b):
            mu = jnp.mean(x, axis=-1, keepdims=True)
            var = jnp.mean(jnp.square(x - mu), axis=-1, keepdims=True)
            return (x - mu) * jax.lax.rsqrt(var + EPS) * w + b
        b, s, h = hidden_states.shape
        normed = _layernorm(hidden_states, ln_w, ln_b)
        xf = normed.reshape(-1, h)
        logits = xf @ router_w
        top_idx = jnp.argmax(logits, axis=-1)
        top_score = jax.nn.sigmoid(jnp.max(logits, axis=-1))

        def body(acc, ew):
            g, u, d, e = ew
            w = jnp.where(top_idx == e, top_score, 0.0)[:, None]
            xe = xf * w
            hmid = jax.nn.silu(xe @ g) * (xe @ u)
            return (acc + hmid @ d, None)
        routed, _ = jax.lax.scan(body, jnp.zeros_like(xf), (gate_w, up_w, down_w, jnp.arange(E)))
        shared = jax.nn.silu(xf @ sh_gate) * (xf @ sh_up) @ sh_down
        moe_out = (routed + shared).reshape(b, s, h)
        return hidden_states + moe_out

    def _L1_attn_ref(x, W_in, conv_w, conv_b, W_x, W_dt, b_dt, A_log, D, W_out):
        import jax, jax.numpy as jnp
        import numpy as np
        BATCH, L, D_MODEL = (2, 128, 128)
        D_STATE, D_CONV, EXPAND = (16, 4, 2)
        D_INNER = EXPAND * D_MODEL
        DT_RANK = max(1, -(-D_MODEL // 16))

        def _forward(x, W_in, conv_w, conv_b, W_x, W_dt, b_dt, A_log, D, W_out):
            xv = x @ W_in
            xc = jnp.transpose(xv, (0, 2, 1))
            xc = jax.lax.conv_general_dilated(xc, conv_w, window_strides=(1,), padding=[(D_CONV - 1, 0)], dimension_numbers=('NCH', 'OIH', 'NCH'), feature_group_count=D_INNER)
            xv = jnp.transpose(xc, (0, 2, 1)) + conv_b
            xv = jax.nn.silu(xv)
            ssm = xv @ W_x
            dt_raw = ssm[..., :DT_RANK]
            Bp = ssm[..., DT_RANK:DT_RANK + D_STATE]
            Cp = ssm[..., DT_RANK + D_STATE:]
            delta = jax.nn.softplus(dt_raw @ W_dt + b_dt)
            A = -jnp.exp(A_log)
            dA = jnp.exp(delta[..., None] * A)
            dBx = delta[..., None] * Bp[:, :, None, :] * xv[..., None]

            def comb(c1, c2):
                a1, b1 = c1
                a2, b2 = c2
                return (a1 * a2, a2 * b1 + b2)
            _, h = jax.lax.associative_scan(comb, (dA, dBx), axis=1)
            y = jnp.einsum('bldn,bln->bld', h, Cp)
            y = y + xv * D
            return y @ W_out
        return _forward(x, W_in, conv_w, conv_b, W_x, W_dt, b_dt, A_log, D, W_out)

    def _L1_ffn_ref(x, w_gate, w_up, w_down):
        import jax, jax.numpy as jnp
        import numpy as np
        DIM = 128
        HIDDEN = 384
        SCALE = 1.0 / 127.0

        def _dequant(w_int, dtype):
            return w_int.astype(dtype) * jnp.asarray(SCALE, dtype)
        wg = _dequant(w_gate, x.dtype)
        wu = _dequant(w_up, x.dtype)
        wd = _dequant(w_down, x.dtype)
        gate = jnp.einsum('bsd,hd->bsh', x, wg)
        up = jnp.einsum('bsd,hd->bsh', x, wu)
        h = jax.nn.silu(gate) * up
        return jnp.einsum('bsh,dh->bsd', h, wd)
    x = L0_attn_x
    xn = _layernorm(x, axis=-1)
    s = _L0_attn_ref(xn, L0_attn_Wq, L0_attn_bq, L0_attn_Wk, L0_attn_bk, L0_attn_Wv, L0_attn_bv, L0_attn_Wo, L0_attn_bo)
    g = _silu(_L0_ffn_ref(xn, L0_ffn_ln_w, L0_ffn_ln_b, L0_ffn_router_w, L0_ffn_gate_w, L0_ffn_up_w, L0_ffn_down_w, L0_ffn_sh_gate, L0_ffn_sh_up, L0_ffn_sh_down))
    x = x + s * g
    xn = _layernorm(x, axis=-1)
    s = _L1_attn_ref(xn, L1_attn_W_in, L1_attn_conv_w, L1_attn_conv_b, L1_attn_W_x, L1_attn_W_dt, L1_attn_b_dt, L1_attn_A_log, L1_attn_D, L1_attn_W_out)
    g = _silu(_L1_ffn_ref(xn, L1_ffn_w_gate, L1_ffn_w_up, L1_ffn_w_down))
    x = x + s * g
    return x

_drawn_inputs = setup_inputs


def setup_inputs(seed=0):
    import zlib

    import numpy as np

    out = dict(_drawn_inputs(seed))
    spreads = {'L0_attn_bq': (0.0, 0.8),
     'L0_attn_bk': (0.0, 0.8),
     'L0_attn_bv': (0.0, 0.1),
     'L0_attn_bo': (0.0, 0.1),
     'L0_ffn_ln_w': (1.0, 0.6),
     'L0_ffn_ln_b': (0.0, 0.8),
     'L1_attn_D': (1.0, 0.2)}
    factors = {'L0_ffn_router_w': 8.0,
     'L0_ffn_gate_w': 8.0,
     'L0_ffn_up_w': 8.0,
     'L0_ffn_down_w': 8.0,
     'L0_ffn_sh_gate': 8.0,
     'L0_ffn_sh_up': 8.0,
     'L0_ffn_sh_down': 8.0,
     'L1_attn_W_x': 64.0,
     'L1_attn_W_dt': 186.925,
     'L1_attn_b_dt': 64.0,
     'L1_attn_A_log': 200.0}
    for name, (base, spread) in spreads.items():
        noise = np.random.default_rng([zlib.crc32(name.encode()), seed]).standard_normal(out[name].shape)
        drawn = base * np.exp(spread * noise) if base else spread * noise
        out[name] = jnp.asarray(drawn.astype(out[name].dtype))
    for name, factor in factors.items():
        out[name] = (out[name] * factor).astype(out[name].dtype)
    return out
```

```python
import concourse.bass as bass
from concourse import mybir
from contextlib import ExitStack


def attention_moe_mamba_ffn(nc, t, out):
    fp32 = mybir.dt.float32
    i32 = mybir.dt.int32
    u32 = mybir.dt.uint32
    ALU = mybir.AluOpType
    ACT = mybir.ActivationFunctionType
    X = mybir.AxisListType.X
    ds = bass.ds

    P = 128
    NB, L, D = t["x"].shape
    TPB = L // P
    NT = NB * TPB
    NE = t["router"].shape[1]
    I = t["gate"].shape[2]
    KI = I // P
    SLOT_TILES = NT + NE
    LN_EPS = 1e-5
    DI = t["W_in"].shape[1]
    KH = DI // P
    NS = t["A_log"].shape[1]
    TAPS = t["conv_w"].shape[1]
    RX = t["W_x"].shape[1]
    RDT = RX - 2 * NS
    HID = t["wg"].shape[1]
    KF = HID // P
    DEQUANT = 1.0 / 127.0
    A_LOG_MAX = 80.0

    ctx = ExitStack()
    with ctx:
        def sb(name, shape, dt=fp32):
            return ctx.enter_context(nc.sbuf_tensor(name, shape, dt))

        def sem(name):
            return ctx.enter_context(nc.semaphore(name))

        xs_dram = nc.dram_tensor("xs_dram", [SLOT_TILES * P, D], fp32, kind="Internal").ap()
        ys_dram = nc.dram_tensor("ys_dram", [SLOT_TILES * P, D], fp32, kind="Internal").ap()
        bt_dram = nc.dram_tensor("bt_dram", [NS, L], fp32, kind="Internal").ap()

        x_all = sb("x_all", [P, NT, D])
        res_all = sb("res_all", [P, NT, D])
        xnT_all = sb("xnT_all", [P, NB * L])
        nfT_all = sb("nfT_all", [P, NB * L])
        nf_all = sb("nf_all", [P, NT, D])
        vo_all = sb("vo_all", [P, NT, D])
        attn_all = sb("attn_all", [P, NT, D])
        const = sb("const", [P, t["const"].shape[1]])
        psum = ctx.enter_context(nc.psum_tensor("psum", [P, 8, 512], fp32))
        stats = sb("stats", [P, NT, 6])
        layer0 = ctx.enter_context(ExitStack())

        def sb(name, shape, dt=fp32):
            return layer0.enter_context(nc.sbuf_tensor(name, shape, dt))

        gu = sb("gu", [P, NE, 2 * I])
        down = sb("down", [P, NE, KI, D])
        shgu = sb("shgu", [P, 2 * I])
        shdown = sb("shdown", [P, KI, D])
        WqT = sb("WqT", [P, D])
        WkT = sb("WkT", [P, D])
        Wv = sb("Wv", [P, D])
        WoT = sb("WoT", [P, D])
        Wvo = sb("Wvo", [P, D])
        vobias = sb("vobias", [P, D])
        cols = sb("cols", [P, 5])
        rows = sb("rows", [P, 3, D])
        router = sb("router", [P, NE])
        ident = const[:, 0:P]
        lower = const[:, P:2 * P]
        ones = const[:, 2 * P:3 * P]
        thr = const[:, 3 * P:3 * P + NT]
        slot_tile = const[:, 3 * P + NT:3 * P + NT + SLOT_TILES]
        eidx = const[:, 3 * P + NT + SLOT_TILES:3 * P + NT + SLOT_TILES + NE]
        bank = [psum[:, i, :] for i in range(8)]

        s_passed = sem("waits_passed")

        def alone(eng):
            eng.sem_inc(s_passed, 1)

        s_w = sem("weights_loaded")
        s_x = [sem(f"x_loaded_{i}") for i in range(NB)]

        mean_r = sb("mean_r", [P, NT])
        rstd1 = sb("rstd1", [P, NT])
        rstd12 = sb("rstd12", [P, NT])
        score = sb("score", [P, NT])
        pos = sb("pos", [P, NT], u32)
        logits = sb("logits", [P, NT, NE])
        guoff = sb("guoff", [P, SLOT_TILES], i32)

        def mean_var(dve, link, mean, var, tmp, st):
            me, mo = st[:, :, 1], st[:, :, 4]
            link(nc.vector.tensor_tensor(mean, me, mo, ALU.add))
            link(nc.vector.tensor_scalar(mean, mean, 0.5, None, ALU.mult))
            link(nc.vector.tensor_tensor(tmp, me, mo, ALU.subtract))
            link(nc.vector.tensor_tensor(tmp, tmp, tmp, ALU.mult))
            link(nc.vector.tensor_tensor(var, st[:, :, 2], st[:, :, 5], ALU.add))
            link(nc.vector.tensor_scalar(var, var, 1.0 / D, None, ALU.mult))
            link(nc.vector.scalar_tensor_tensor(var, tmp, 0.25, var, ALU.mult, ALU.add))

        with ExitStack() as ph:
            def sb1(name, shape, dt=fp32):
                return ph.enter_context(nc.sbuf_tensor(name, shape, dt))
            var = sb1("var", [P, NT])
            tmp = sb1("tmp", [P, NT])
            std = sb1("std", [P, NT])
            xn_w = sb1("xn_w", [P, TPB, D])
            z_w = sb1("z_w", [P, TPB, D])
            zw_w = sb1("zw_w", [P, TPB, D])
            xnT_w = sb1("xnT_w", [P, L])
            nfT_w = sb1("nfT_w", [P, L])
            zeros = sb1("zeros", [P, SLOT_TILES * D // 4])
            bvb = sb1("bvb", [P, P])
            names = {"xn_done": 1, "z_done": 1, "xT_ps": 1, "zT_ps": 1, "xnT_w_done": 1, "nfT_w_done": 1,
                     "vo_ps": 1, "logit_ps": 1, "vo_done": 1, "logit_done": 1, "xnT_copied": 1,
                     "xn_copied": 1, "nfT_copied": 1, "zw": 1, "nf": 1}
            S = {n: sem("p1_" + n) for n in names}
            s_dve = sem("p1_dve_step")
            s_var = sem("p1_var_ready")
            s_std = sem("p1_std_ready")
            s_zero = sem("p1_zeros_ready")
            s_zd = sem("p1_slots_zeroed")
            s_bvb = sem("p1_bv_broadcast")
            s_wvo = sem("p1_wvo_ps")
            s_wvo_sb = sem("p1_wvo_sb")

            def at(b, n, c=1):
                return (b + 1) * names[n] + c

            block = ph.enter_context(nc.Block())

            @block.sync
            def _(sp):
                for b in range(NB):
                    sp.dma_start(x_all[:, b * TPB:(b + 1) * TPB, :],
                                 t["x"][b].rearrange("(j p) d -> p j d", p=P)).then_inc(s_x[b], 16)
                sp.dma_start(gu[:, :, 0:I], t["gate"].rearrange("e h i -> h e i")).then_inc(s_w, 16)
                sp.dma_start(gu[:, :, I:2 * I], t["up"].rearrange("e h i -> h e i")).then_inc(s_w, 16)
                sp.dma_start(down[:, :, :, :], t["down"].rearrange("e (k p) h -> p e k h", p=P)).then_inc(s_w, 16)
                sp.wait_ge(s_zero, 1)
                z4 = xs_dram.rearrange("(a p r) d -> a p (r d)", a=4, p=P)
                for a in range(4):
                    sp.dma_start(z4[a], zeros[:, :]).then_inc(s_zd, 16)
                sp.wait_ge(s_zd, 64)

            @block.scalar
            def _(act):
                loads = [(const[:, :], t["const"]), (WqT[:, :], t["WqT"]), (WkT[:, :], t["WkT"]),
                         (Wv[:, :], t["Wv"]), (WoT[:, :], t["WoT"]), (router[:, :], t["router"]),
                         (shgu[:, 0:I], t["sh_gate"]), (shgu[:, I:2 * I], t["sh_up"]),
                         (shdown[:, :, :], t["sh_down"].rearrange("(k p) h -> p k h", p=P))]
                loads += [(cols[:, i:i + 1], t[n].rearrange("(p a) -> p a", a=1))
                          for i, n in enumerate(("bq", "bk", "ln_w", "ln_b", "bv"))]
                loads += [(rows[:, i, :], t[n].rearrange("(a d) -> a d", a=1).to_broadcast([P, D]))
                          for i, n in enumerate(("bo", "ln_w", "ln_b"))]
                for dst, src in loads:
                    act.dma_start(dst, src).then_inc(s_w, 16)
                act.wait_ge(s_var, 1)
                nc.scalar.activation(std[:, :], var[:, :], ACT.Sqrt).then_inc(s_std, 1)
                act.wait_ge(s_var, 2)
                nc.scalar.activation(tmp[:, :], var[:, :], ACT.Sqrt).then_inc(s_std, 1)
                act.wait_ge(s_w, 16 * 20)
                with act.Fori(0, NB) as b:
                    act.wait_ge(S["xT_ps"], at(b, "xT_ps"))
                    act.wait_ge(S["vo_ps"], at(b, "vo_ps", 0))
                    act.wait_ge(S["xnT_copied"], at(b, "xnT_copied", 0))
                    nc.scalar.activation(xnT_w[:, :], bank[0], ACT.Copy).then_inc(S["xnT_w_done"], 1)
                    act.wait_ge(S["zT_ps"], at(b, "zT_ps"))
                    act.wait_ge(S["logit_ps"], at(b, "logit_ps", 0))
                    act.wait_ge(S["nfT_copied"], at(b, "nfT_copied", 0))
                    nc.scalar.activation(nfT_w[:, :], bank[1], ACT.Identity, bias=cols[:, 3:4],
                                         scale=cols[:, 2:3]).then_inc(S["nfT_w_done"], 1)
                    act.wait_ge(S["nfT_w_done"], at(b, "nfT_w_done"))
                    nc.scalar.activation(nfT_all[:, ds(b * L, L)], nfT_w[:, :], ACT.Copy).then_inc(S["nfT_copied"], 1)

            @block.gpsimd
            def _(pool):
                nc.gpsimd.memset(zeros[:, :], 0.0).then_inc(s_zero, 1)
                for n, per in names.items():
                    pool.sem_inc(S[n], per)
                with pool.Fori(0, NB) as b:
                    pool.wait_ge(S["xn_done"], at(b, "xn_done"))
                    nc.gpsimd.tensor_copy(res_all[:, ds(b * TPB, TPB), :], xn_w[:, :, :]).then_inc(S["xn_copied"], 1)
                    pool.wait_ge(S["xnT_w_done"], at(b, "xnT_w_done"))
                    nc.gpsimd.tensor_copy(xnT_all[:, ds(b * L, L)], xnT_w[:, :]).then_inc(S["xnT_copied"], 1)

            @block.tensor
            def _(pe):
                pe.wait_ge(s_w, 16 * 20)
                nc.tensor.matmul(bank[4][:, 0:D], Wv[:, :], WoT[:, :], start=True, stop=True)
                pe.wait_ge(s_bvb, 1)
                nc.tensor.matmul(bank[4][:, D:2 * D], bvb[:, :], WoT[:, :], start=True, stop=True).then_inc(s_wvo, 1)
                pe.wait_ge(s_wvo_sb, 1)
                with pe.Fori(0, NB) as b:
                    pe.wait_ge(S["xn_done"], at(b, "xn_done"))
                    pe.wait_ge(S["xnT_w_done"], at(b, "xnT_w_done", 0))
                    for j in range(TPB):
                        ins = nc.tensor.transpose(bank[0][:, j * P:(j + 1) * P], xn_w[:, j, :], ident)
                    ins.then_inc(S["xT_ps"], 1)
                    pe.wait_ge(S["z_done"], at(b, "z_done"))
                    pe.wait_ge(S["nfT_w_done"], at(b, "nfT_w_done", 0))
                    for j in range(TPB):
                        ins = nc.tensor.transpose(bank[1][:, j * P:(j + 1) * P], z_w[:, j, :], ident)
                    ins.then_inc(S["zT_ps"], 1)
                    pe.wait_ge(S["xnT_w_done"], at(b, "xnT_w_done"))
                    pe.wait_ge(S["vo_done"], at(b, "vo_done", 0))
                    for j in range(TPB):
                        ins = nc.tensor.matmul(bank[2][:, j * P:(j + 1) * P], xnT_w[:, j * P:(j + 1) * P], Wvo[:, :],
                                               start=True, stop=True)
                    ins.then_inc(S["vo_ps"], 1)
                    pe.wait_ge(S["nfT_w_done"], at(b, "nfT_w_done"))
                    pe.wait_ge(S["logit_done"], at(b, "logit_done", 0))
                    for j in range(TPB):
                        ins = nc.tensor.matmul(bank[3][:, j * NE:(j + 1) * NE], nfT_w[:, j * P:(j + 1) * P],
                                               router[:, :], start=True, stop=True)
                    ins.then_inc(S["logit_ps"], 1)

            @block.vector
            def _(dve):
                n = [0]

                def link(ins):
                    n[0] += 1
                    ins.then_inc(s_dve, 1)
                    dve.wait_ge(s_dve, n[0])

                for b in range(NB):
                    dve.wait_ge(s_x[b], 16)
                    for j in range(TPB):
                        ins = nc.vector.bn_stats(stats[:, b * TPB + j, :], x_all[:, b * TPB + j, :])
                link(ins)
                mean_var(dve, link, mean_r[:, :], var[:, :], tmp[:, :], stats)
                nc.vector.tensor_copy(rstd12[:, :], var[:, :])
                link(nc.vector.tensor_scalar(std[:, :], var[:, :], 1.0, None, ALU.mult))
                link(nc.vector.tensor_scalar(var[:, :], var[:, :], LN_EPS, None, ALU.add))
                nc.vector.tensor_copy(rstd1[:, :], var[:, :]).then_inc(s_var, 1)
                dve.wait_ge(s_std, 1)
                link(nc.vector.reciprocal(rstd1[:, :], std[:, :]))
                link(nc.vector.tensor_tensor(var[:, :], rstd1[:, :], rstd1[:, :], ALU.mult))
                link(nc.vector.tensor_tensor(var[:, :], var[:, :], rstd12[:, :], ALU.mult))
                nc.vector.tensor_scalar(var[:, :], var[:, :], LN_EPS, None, ALU.add).then_inc(s_var, 1)
                dve.wait_ge(s_std, 2)
                link(nc.vector.reciprocal(tmp[:, :], tmp[:, :]))
                link(nc.vector.tensor_tensor(rstd12[:, :], tmp[:, :], rstd1[:, :], ALU.mult))
                dve.wait_ge(s_w, 16 * 20)
                link(nc.vector.memset(bvb[:, :], 1.0))
                nc.vector.tensor_scalar(bvb[:, :], bvb[:, :], cols[:, 4:5], None, ALU.mult).then_inc(s_bvb, 1)
                dve.wait_ge(s_wvo, 1)
                nc.vector.tensor_copy(Wvo[:, :], bank[4][:, 0:D])
                link(nc.vector.tensor_tensor(vobias[:, :], bank[4][:, D:2 * D], rows[:, 0, :], ALU.add))
                dve.sem_inc(s_wvo_sb, 1)
                with dve.Fori(0, NB) as b:
                    dve.wait_ge(S["xT_ps"], at(b, "xT_ps", 0))
                    dve.wait_ge(S["xn_copied"], at(b, "xn_copied", 0))
                    for j in range(TPB):
                        ins = nc.vector.tensor_scalar(xn_w[:, j, :], x_all[:, ds(b * TPB + j, 1), :],
                                                      mean_r[:, ds(b * TPB + j, 1)], rstd1[:, ds(b * TPB + j, 1)],
                                                      ALU.subtract, ALU.mult)
                    ins.then_inc(S["xn_done"], 1)
                    dve.wait_ge(S["zT_ps"], at(b, "zT_ps", 0))
                    dve.wait_ge(S["zw"], at(b, "zw", 0))
                    for j in range(TPB):
                        ins = nc.vector.tensor_scalar(z_w[:, j, :], x_all[:, ds(b * TPB + j, 1), :],
                                                      mean_r[:, ds(b * TPB + j, 1)], rstd12[:, ds(b * TPB + j, 1)],
                                                      ALU.subtract, ALU.mult)
                    ins.then_inc(S["z_done"], 1)
                    dve.wait_ge(S["z_done"], at(b, "z_done"))
                    dve.wait_ge(S["nf"], at(b, "nf", 0))
                    nc.vector.tensor_tensor(zw_w[:, :, :], z_w[:, :, :], rows[:, 1:2, :].to_broadcast([P, TPB, D]),
                                            ALU.mult).then_inc(S["zw"], 1)
                    dve.wait_ge(S["zw"], at(b, "zw"))
                    nc.vector.tensor_tensor(nf_all[:, ds(b * TPB, TPB), :], zw_w[:, :, :],
                                            rows[:, 2:3, :].to_broadcast([P, TPB, D]), ALU.add).then_inc(S["nf"], 1)
                    dve.wait_ge(S["vo_ps"], at(b, "vo_ps"))
                    nc.vector.tensor_tensor(vo_all[:, ds(b * TPB, TPB), :],
                                            bank[2].rearrange("p (j d) -> p j d", d=D),
                                            vobias[:, None, :].to_broadcast([P, TPB, D]), ALU.add)\
                        .then_inc(S["vo_done"], 1)
                    dve.wait_ge(S["logit_ps"], at(b, "logit_ps"))
                    nc.vector.tensor_copy(logits[:, ds(b * TPB, TPB), :],
                                          bank[3][:, 0:TPB * NE].rearrange("p (j e) -> p j e", e=NE))\
                        .then_inc(S["logit_done"], 1)

        with ExitStack() as ph:
            def sb2(name, shape, dt=fp32):
                return ph.enter_context(nc.sbuf_tensor(name, shape, dt))
            top = sb2("top", [P, NT])
            eq = sb2("eq", [P, NT, NE])
            first = sb2("first", [P, NT])
            onehot = sb2("onehot", [P, NE, NT])
            cnt = sb2("cnt", [P, NE, NT])
            cum = sb2("cum", [P, NE, NT])
            big = sb2("big", [P, SLOT_TILES, NE])
            tot = sb2("tot", [P, NE])
            ntile = sb2("ntile", [P, NE])
            tend = sb2("tend", [P, NE])
            base = sb2("base", [P, NE])
            slot = sb2("slot", [P, NE, NT])
            posf = sb2("posf", [P, NT])
            exf = sb2("exf", [P, SLOT_TILES])
            s_oh = sem("p2_onehot_ready")
            s_cnt = sem("p2_counts_ps")
            s_top = sem("p2_top_ready")
            s_tanh = sem("p2_tanh_ready")
            s_dve2 = sem("p2_dve_step")
            block = ph.enter_context(nc.Block())

            @block.tensor
            def _(pe):
                pe.wait_ge(s_oh, 1)
                oh = onehot[:, :, :].rearrange("p e j -> p (e j)")
                nc.tensor.matmul(bank[0][:, 0:NE * NT], ones, oh, start=True, stop=True)
                nc.tensor.matmul(bank[1][:, 0:NE * NT], lower, oh, start=True, stop=True).then_inc(s_cnt, 1)

            @block.scalar
            def _(act):
                act.wait_ge(s_top, 1)
                nc.scalar.activation(score[:, :], top[:, :], ACT.Tanh, scale=0.5).then_inc(s_tanh, 1)

            @block.vector
            def _(dve):
                n = [0]

                def link(ins):
                    n[0] += 1
                    ins.then_inc(s_dve2, 1)
                    dve.wait_ge(s_dve2, n[0])

                link(nc.vector.tensor_reduce(top[:, :], logits[:, :, :], X, ALU.max))
                link(nc.vector.tensor_tensor(eq[:, :, :], logits[:, :, :],
                                             top[:, :, None].to_broadcast([P, NT, NE]), ALU.is_equal))
                dve.sem_inc(s_top, 1)
                link(nc.vector.tensor_tensor(eq[:, :, :], eq[:, :, :],
                                             eidx[:, None, :].to_broadcast([P, NT, NE]), ALU.mult))
                link(nc.vector.tensor_reduce(first[:, :], eq[:, :, :], X, ALU.min))
                link(nc.vector.tensor_tensor(onehot[:, :, :], first[:, None, :].to_broadcast([P, NE, NT]),
                                             eidx[:, :, None].to_broadcast([P, NE, NT]), ALU.is_equal))
                dve.sem_inc(s_oh, 1)
                dve.wait_ge(s_tanh, 1)
                nc.vector.tensor_scalar(score[:, :], score[:, :], 0.5, 0.5, ALU.mult, ALU.add)
                dve.wait_ge(s_cnt, 1)
                link(nc.vector.tensor_copy(cnt[:, :, :], bank[0][:, 0:NE * NT].rearrange("p (e j) -> p e j", e=NE)))
                link(nc.vector.tensor_reduce(tot[:, :], cnt[:, :, :], X, ALU.add))
                link(nc.vector.tensor_tensor_scan(cum[:, :, :].rearrange("p e j -> p (e j)"),
                                                  cnt[:, :, :].rearrange("p e j -> p (e j)"),
                                                  cnt[:, :, :].rearrange("p e j -> p (e j)"),
                                                  0.0, ALU.add, ALU.bypass))
                link(nc.vector.tensor_tensor(slot[:, :, :], tot[:, :, None].to_broadcast([P, NE, NT]),
                                             thr[:, None, :].to_broadcast([P, NE, NT]), ALU.is_gt))
                link(nc.vector.tensor_reduce(ntile[:, :], slot[:, :, :], X, ALU.add))
                link(nc.vector.tensor_tensor_scan(tend[:, :], ntile[:, :], ntile[:, :], 0.0, ALU.add, ALU.bypass))
                link(nc.vector.tensor_tensor(base[:, :], tend[:, :], ntile[:, :], ALU.subtract))
                link(nc.vector.tensor_scalar(base[:, :], base[:, :], float(P), None, ALU.mult))
                link(nc.vector.tensor_tensor(base[:, :], base[:, :], cum[:, :, NT - 1], ALU.subtract))
                link(nc.vector.tensor_tensor(base[:, :], base[:, :], tot[:, :], ALU.add))
                link(nc.vector.tensor_tensor(slot[:, :, :], cum[:, :, :], cnt[:, :, :], ALU.subtract))
                link(nc.vector.tensor_tensor(slot[:, :, :], slot[:, :, :],
                                             base[:, :, None].to_broadcast([P, NE, NT]), ALU.add))
                link(nc.vector.tensor_tensor(slot[:, :, :], slot[:, :, :],
                                             bank[1][:, 0:NE * NT].rearrange("p (e j) -> p e j", e=NE), ALU.add))
                link(nc.vector.tensor_tensor(slot[:, :, :], slot[:, :, :], onehot[:, :, :], ALU.mult))
                link(nc.vector.tensor_reduce(posf[:, :], slot[:, :, :].rearrange("p e j -> p j e"), X, ALU.add))
                nc.vector.tensor_copy(pos[:, :], posf[:, :])
                link(nc.vector.tensor_tensor(big[:, :, :], slot_tile[:, :, None].to_broadcast([P, SLOT_TILES, NE]),
                                             tend[:, None, :].to_broadcast([P, SLOT_TILES, NE]), ALU.is_ge))
                link(nc.vector.tensor_reduce(exf[:, :], big[:, :, :], X, ALU.add))
                link(nc.vector.tensor_scalar(exf[:, :], exf[:, :], float(NE - 1), None, ALU.min))
                link(nc.vector.tensor_copy(guoff[:, :], exf[:, :]))

        with ExitStack() as ph:
            def sb3(name, shape, dt=fp32):
                return ph.enter_context(nc.sbuf_tensor(name, shape, dt))
            q_w = sb3("q_w", [P, L])
            k_w = sb3("k_w", [P, L])
            T2 = sb3("T2", [P, 2, L])
            T1 = sb3("T1", [P, 2, L])
            U = sb3("U", [P, L])
            W = sb3("W", [P, 2, L])
            PR = sb3("PR", [P, 2, L])
            PT = sb3("PT", [P, 2, TPB, P])
            wmax = sb3("wmax", [P, TPB])
            nbias = sb3("nbias", [P, TPB])
            rsum = sb3("rsum", [P, TPB])
            rinv = sb3("rinv", [P, TPB])
            sht = sb3("sht", [P, L])
            sha = sb3("sha", [P, L])
            shh = sb3("shh", [P, KI, L])
            xs_w = sb3("xs_w", [P, 2, TPB, D])
            pos_w = sb3("pos_w", [P, 2, TPB], u32)
            names = {"q_ps": 1, "k_ps": 1, "q_sb": 1, "k_sb": 1, "s_ps": TPB, "t2": TPB, "t1": TPB, "u": TPB,
                     "w": TPB, "mx": TPB, "nb": TPB, "p": TPB, "pT_ps": TPB, "pT_sb": TPB, "o_ps": TPB,
                     "rinv": 1, "attn": 1, "shg_ps": KI, "sht": KI, "sha": KI, "shh": KI, "shd_ps": 1, "res": 1}
            S = {n: sem("p3_" + n) for n in names}
            s_xs = [sem(f"p3_xs_ready_{i}") for i in range(2)]
            s_pw = [sem(f"p3_pos_ready_{i}") for i in range(2)]
            s_sc = [sem(f"p3_scattered_{i}") for i in range(2)]
            s_cr = sem("p3_credits_given")

            def at(b, n, c):
                return (b + 1) * names[n] + c

            block = ph.enter_context(nc.Block())

            @block.gpsimd
            def _(pool):
                for n, per in names.items():
                    pool.sem_inc(S[n], per)
                with pool.Fori(0, NB // 2) as b2:
                    for i in range(2):
                        nc.gpsimd.tensor_copy(pos_w[:, i, :], pos[:, ds((b2 * 2 + i) * TPB, TPB)]).then_inc(s_pw[i], 1)
                        nc.gpsimd.tensor_tensor(xs_w[:, i, :, :], nf_all[:, ds((b2 * 2 + i) * TPB, TPB), :],
                                                score[:, ds((b2 * 2 + i) * TPB, TPB), None]
                                                .to_broadcast([P, TPB, D]), ALU.mult).then_inc(s_xs[i], 1)
                        pool.wait_ge(s_pw[i], b2 + 1)
                        pool.wait_ge(s_xs[i], b2 + 1)
                        alone(pool)
                        for j in range(TPB):
                            pool.indirect_dma_start(
                                xs_dram, bass.IndirectOffsetOnAxis(ap=pos_w[:, i, j:j + 1], axis=0),
                                xs_w[:, i, j, :], None).then_inc(s_sc[i], 16)
                    for i in range(2):
                        pool.wait_ge(s_sc[i], (b2 + 1) * 16 * TPB)

            @block.tensor
            def _(pe):
                with pe.Fori(0, NB) as b:
                    def w(n, c):
                        pe.wait_ge(S[n], at(b, n, c))

                    def scores(j):
                        w("u", j + 1 - 2)
                        nc.tensor.matmul(bank[j % 2], q_w[:, j * P:(j + 1) * P], k_w[:, :], start=True, stop=True)\
                            .then_inc(S["s_ps"], 1)

                    def shared_up(k):
                        w("shh", k)
                        nc.tensor.matmul(bank[5], shgu[:, k * P:(k + 1) * P], nfT_all[:, ds(b * L, L)],
                                         start=True, stop=True)
                        nc.tensor.matmul(bank[6], shgu[:, I + k * P:I + (k + 1) * P], nfT_all[:, ds(b * L, L)],
                                         start=True, stop=True).then_inc(S["shg_ps"], 1)

                    def turn(j):
                        w("p", j + 1)
                        w("pT_sb", j + 1 - 2)
                        for c in range(TPB):
                            ins = nc.tensor.transpose(bank[2 + j % 2][:, c * P:(c + 1) * P],
                                                      PR[:, j % 2, c * P:(c + 1) * P], ident)
                        ins.then_inc(S["pT_ps"], 1)

                    def values(j):
                        w("pT_sb", j + 1)
                        if j == 0:
                            w("attn", 0)
                        for c in range(TPB):
                            ins = nc.tensor.matmul(bank[4][:, j * P:(j + 1) * P], PT[:, j % 2, c, :],
                                                   vo_all[:, ds(b * TPB + c, 1), :],
                                                   start=(c == 0), stop=(c == TPB - 1))
                        ins.then_inc(S["o_ps"], 1)

                    w("shh", 0)
                    nc.tensor.matmul(bank[5], WqT[:, :], xnT_all[:, ds(b * L, L)], start=True, stop=True)\
                        .then_inc(S["q_ps"], 1)
                    nc.tensor.matmul(bank[6], WkT[:, :], xnT_all[:, ds(b * L, L)], start=True, stop=True)\
                        .then_inc(S["k_ps"], 1)
                    w("q_sb", 1)
                    w("k_sb", 1)
                    scores(0)
                    scores(1)
                    shared_up(0)
                    turn(0)
                    scores(2)
                    values(0)
                    shared_up(1)
                    turn(1)
                    scores(3)
                    values(1)
                    turn(2)
                    values(2)
                    w("shh", KI)
                    w("res", 0)
                    for j in range(TPB):
                        for k in range(KI):
                            ins = nc.tensor.matmul(bank[7][:, j * P:(j + 1) * P], shh[:, k, j * P:(j + 1) * P],
                                                   shdown[:, k, :], start=(k == 0), stop=(k == KI - 1))
                    ins.then_inc(S["shd_ps"], 1)
                    turn(3)
                    values(3)

            @block.scalar
            def _(act):
                with act.Fori(0, NB) as b:
                    def w(n, c):
                        act.wait_ge(S[n], at(b, n, c))

                    def tanhs(j):
                        w("s_ps", j + 1)
                        w("u", j + 1 - 2)
                        nc.scalar.activation(T2[:, j % 2, :], bank[j % 2], ACT.Tanh, scale=0.5).then_inc(S["t2"], 1)
                        w("w", j + 1 - 2)
                        nc.scalar.activation(T1[:, j % 2, :], bank[j % 2], ACT.Tanh).then_inc(S["t1"], 1)

                    def probs(j):
                        w("nb", j + 1)
                        w("pT_ps", j + 1 - 2)
                        if j == 0:
                            w("rinv", 0)
                        nc.scalar.activation(PR[:, j % 2, :], W[:, j % 2, :], ACT.Exp, bias=nbias[:, j:j + 1],
                                             scale=0.1, accum_out=rsum[:, j:j + 1]).then_inc(S["p"], 1)

                    def turned(j):
                        w("pT_ps", j + 1)
                        w("o_ps", j + 1 - 2)
                        nc.scalar.activation(PT[:, j % 2, :, :], bank[2 + j % 2].rearrange("p (c s) -> p c s", s=P),
                                             ACT.Copy).then_inc(S["pT_sb"], 1)

                    def shared(k):
                        w("shg_ps", k + 1)
                        w("sha", k)
                        nc.scalar.activation(sht[:, :], bank[5], ACT.Tanh, scale=0.5).then_inc(S["sht"], 1)

                    w("k_ps", 1)
                    w("s_ps", 0)
                    nc.scalar.activation(k_w[:, :], bank[6], ACT.Identity, bias=cols[:, 1:2]).then_inc(S["k_sb"], 1)
                    tanhs(0)
                    tanhs(1)
                    probs(0)
                    shared(0)
                    turned(0)
                    tanhs(2)
                    probs(1)
                    shared(1)
                    turned(1)
                    tanhs(3)
                    probs(2)
                    turned(2)
                    probs(3)
                    turned(3)

            @block.vector
            def _(dve):
                with dve.Fori(0, NB) as b:
                    def w(n, c):
                        dve.wait_ge(S[n], at(b, n, c))

                    def theta(j):
                        w("t2", j + 1)
                        w("t1", j + 1)
                        w("w", j)
                        nc.vector.scalar_tensor_tensor(U[:, :], bank[j % 2], 0.0, T2[:, j % 2, :], ALU.max, ALU.add)\
                            .then_inc(S["u"], 1)
                        w("u", j + 1)
                        w("p", j + 1 - 2)
                        w("mx", j + 1 - 2)
                        nc.vector.scalar_tensor_tensor(W[:, j % 2, :], T1[:, j % 2, :], 1.5, U[:, :],
                                                       ALU.mult, ALU.add).then_inc(S["w"], 1)
                        w("w", j + 1)
                        w("nb", j + 1 - TPB)
                        nc.vector.tensor_reduce(wmax[:, j:j + 1], W[:, j % 2, :], X, ALU.max).then_inc(S["mx"], 1)
                        w("mx", j + 1)
                        w("p", j + 1 - TPB)
                        nc.vector.tensor_scalar(nbias[:, j:j + 1], wmax[:, j:j + 1], -0.1, None, ALU.mult)\
                            .then_inc(S["nb"], 1)

                    def shared(k):
                        w("sht", k + 1)
                        w("shh", k)
                        nc.vector.scalar_tensor_tensor(sha[:, :], sht[:, :], 1.0, bank[5], ALU.add, ALU.mult)\
                            .then_inc(S["sha"], 1)
                        w("sha", k + 1)
                        w("shd_ps", 0)
                        nc.vector.scalar_tensor_tensor(shh[:, k, :], sha[:, :], 0.5, bank[6], ALU.mult, ALU.mult)\
                            .then_inc(S["shh"], 1)

                    w("q_ps", 1)
                    w("s_ps", 0)
                    nc.vector.tensor_scalar(q_w[:, :], bank[5], cols[:, 0:1], None, ALU.add).then_inc(S["q_sb"], 1)
                    theta(0)
                    theta(1)
                    shared(0)
                    theta(2)
                    shared(1)
                    theta(3)
                    w("shd_ps", 1)
                    nc.vector.tensor_tensor(res_all[:, ds(b * TPB, TPB), :], res_all[:, ds(b * TPB, TPB), :],
                                            bank[7].rearrange("p (j d) -> p j d", d=D), ALU.add).then_inc(S["res"], 1)
                    w("p", TPB)
                    w("attn", 0)
                    nc.vector.reciprocal(rinv[:, :], rsum[:, :]).then_inc(S["rinv"], 1)
                    w("rinv", 1)
                    w("o_ps", TPB)
                    nc.vector.tensor_tensor(attn_all[:, ds(b * TPB, TPB), :],
                                            bank[4].rearrange("p (j d) -> p j d", d=D),
                                            rinv[:, :, None].to_broadcast([P, TPB, D]), ALU.mult).then_inc(S["attn"], 1)

        with ExitStack() as ph:
            def sb4(name, shape, dt=fp32):
                return ph.enter_context(nc.sbuf_tensor(name, shape, dt))
            UN = 4
            ROUNDS = SLOT_TILES // UN
            xs_t = sb4("xs_t", [P, UN, D])
            xT = sb4("xT", [P, 2, P])
            th = sb4("th", [P, 2, I])
            ha = sb4("ha", [P, I])
            hm = sb4("hm", [P, 2, I])
            hT = sb4("hT", [P, 2, KI, P])
            yt = sb4("yt", [P, UN, D])
            names = {n: UN for n in ("xT_ps", "xT", "gu_ps", "th", "ha", "hm", "hT_ps", "hT", "y_ps", "y")}
            S = {n: sem("p4_" + n) for n in names}
            s_in = [sem(f"p4_slots_loaded_{i}") for i in range(UN)]
            s_out = [sem(f"p4_slots_stored_{i}") for i in range(UN)]
            gu_flat = gu[:, :, :].rearrange("p e i -> p (e i)")
            down_flat = down[:, :, :, :].rearrange("p e k d -> p (e k d)")

            def at(r, n, c):
                return (r + 1) * names[n] + c

            def slots(dram, r, u):
                return dram[ds((r * UN + u) * P, P), :]

            block = ph.enter_context(nc.Block())

            @block.sync
            def _(sp):
                for u in range(UN):
                    sp.dma_start(xs_t[:, u, :], slots(xs_dram, 0, u)).then_inc(s_in[u], 16)
                with sp.Fori(0, ROUNDS - 1) as r:
                    for u in range(UN):
                        sp.wait_ge(S["xT_ps"], at(r, "xT_ps", u + 1))
                        sp.dma_start(xs_t[:, u, :], slots(xs_dram, r + 1, u)).then_inc(s_in[u], 16)
                        sp.wait_ge(S["y"], at(r, "y", u + 1))
                        sp.dma_start(slots(ys_dram, r, u), yt[:, u, :]).then_inc(s_out[u], 16)
                for u in range(UN):
                    sp.wait_ge(S["y"], at(ROUNDS - 1, "y", u + 1))
                    sp.dma_start(slots(ys_dram, ROUNDS - 1, u), yt[:, u, :]).then_inc(s_out[u], 16)
                for u in range(UN):
                    sp.wait_ge(s_out[u], 16 * (ROUNDS + 1))

            @block.gpsimd
            def _(pool):
                for n, per in names.items():
                    pool.sem_inc(S[n], per)
                for u in range(UN):
                    pool.sem_inc(s_out[u], 16)

            @block.tensor
            def _(pe):
                def turn_x(r, u):
                    pe.wait_ge(s_in[u % UN], 16 * (r + u // UN + 1))
                    pe.wait_ge(S["xT"], at(r, "xT", u + 1 - 2))
                    nc.tensor.transpose(bank[u % 2][:, 0:P], xs_t[:, u % UN, :], ident).then_inc(S["xT_ps"], 1)

                def up(r, u):
                    pe.wait_ge(S["xT"], at(r, "xT", u + 1))
                    pe.wait_ge(S["hm"], at(r, "hm", u + 1 - 2))
                    alone(pe)
                    e = pe.value_load(guoff[0:1, ds(r * UN + u, 1)], min_val=0, max_val=NE - 1)
                    nc.tensor.matmul(bank[2 + u % 2], xT[:, u % 2, :], gu_flat[:, ds(e * (2 * I), 2 * I)],
                                     start=True, stop=True).then_inc(S["gu_ps"], 1)

                def turn_h(r, u):
                    pe.wait_ge(S["hm"], at(r, "hm", u + 1))
                    pe.wait_ge(S["hT"], at(r, "hT", u + 1 - 2))
                    for k in range(KI):
                        ins = nc.tensor.transpose(bank[4 + u % 2][:, k * P:(k + 1) * P],
                                                  hm[:, u % 2, k * P:(k + 1) * P], ident)
                    ins.then_inc(S["hT_ps"], 1)

                def dn(r, u):
                    pe.wait_ge(S["hT"], at(r, "hT", u + 1))
                    pe.wait_ge(S["y"], at(r, "y", u + 1 - 2))
                    alone(pe)
                    e = pe.value_load(guoff[0:1, ds(r * UN + u, 1)], min_val=0, max_val=NE - 1)
                    for k in range(KI):
                        ins = nc.tensor.matmul(bank[6 + u % 2][:, 0:D], hT[:, u % 2, k, :],
                                               down_flat[:, ds(e * (KI * D) + k * D, D)],
                                               start=(k == 0), stop=(k == KI - 1))
                    ins.then_inc(S["y_ps"], 1)

                def steps(r, first, last):
                    for u in range(UN):
                        if not (last and u == UN - 1):
                            up(r, u + 1)
                        if not (first and u == 0):
                            dn(r, u - 1)
                        turn_h(r, u)
                        if not (last and u >= UN - 2):
                            turn_x(r, u + 2)

                turn_x(0, 0)
                turn_x(0, 1)
                up(0, 0)
                steps(0, True, False)
                with pe.Fori(1, ROUNDS - 1) as r:
                    steps(r, False, False)
                steps(ROUNDS - 1, False, True)
                dn(ROUNDS - 1, UN - 1)

            @block.scalar
            def _(act):
                def x_out(r, u):
                    act.wait_ge(S["xT_ps"], at(r, "xT_ps", u + 1))
                    act.wait_ge(S["gu_ps"], at(r, "gu_ps", u + 1 - 2))
                    nc.scalar.activation(xT[:, u % 2, :], bank[u % 2][:, 0:P], ACT.Copy).then_inc(S["xT"], 1)

                def tanh(r, u):
                    act.wait_ge(S["gu_ps"], at(r, "gu_ps", u + 1))
                    act.wait_ge(S["ha"], at(r, "ha", u + 1 - 2))
                    nc.scalar.activation(th[:, u % 2, :], bank[2 + u % 2][:, 0:I], ACT.Tanh, scale=0.5)\
                        .then_inc(S["th"], 1)

                x_out(0, 0)
                x_out(0, 1)
                with act.Fori(0, ROUNDS - 1) as r:
                    for u in range(UN):
                        tanh(r, u)
                        x_out(r, u + 2)
                for u in range(UN):
                    tanh(ROUNDS - 1, u)
                    if u + 2 < UN:
                        x_out(ROUNDS - 1, u + 2)

            @block.vector
            def _(dve):
                def hidden(r, u):
                    dve.wait_ge(S["th"], at(r, "th", u + 1))
                    dve.wait_ge(S["hm"], at(r, "hm", u))
                    nc.vector.scalar_tensor_tensor(ha[:, :], th[:, u % 2, :], 1.0, bank[2 + u % 2][:, 0:I],
                                                   ALU.add, ALU.mult).then_inc(S["ha"], 1)
                    dve.wait_ge(S["ha"], at(r, "ha", u + 1))
                    dve.wait_ge(S["hT_ps"], at(r, "hT_ps", u + 1 - 2))
                    nc.vector.scalar_tensor_tensor(hm[:, u % 2, :], ha[:, :], 0.5, bank[2 + u % 2][:, I:2 * I],
                                                   ALU.mult, ALU.mult).then_inc(S["hm"], 1)

                def h_out(r, u):
                    dve.wait_ge(S["hT_ps"], at(r, "hT_ps", u + 1))
                    dve.wait_ge(S["y_ps"], at(r, "y_ps", u + 1 - 2))
                    nc.vector.tensor_copy(hT[:, u % 2, :, :],
                                          bank[4 + u % 2][:, 0:KI * P].rearrange("p (k s) -> p k s", s=P))\
                        .then_inc(S["hT"], 1)

                def y_out(r, u):
                    dve.wait_ge(S["y_ps"], at(r, "y_ps", u + 1))
                    dve.wait_ge(s_out[u % UN], 16 * (r + 1 + (u - u % UN) // UN))
                    nc.vector.tensor_copy(yt[:, u % UN, :], bank[6 + u % 2][:, 0:D]).then_inc(S["y"], 1)

                def steps(r, first):
                    for u in range(UN):
                        hidden(r, u)
                        if not (first and u == 0):
                            y_out(r, u - 1)
                        h_out(r, u)

                steps(0, True)
                with dve.Fori(1, ROUNDS) as r:
                    steps(r, False)
                y_out(ROUNDS - 1, UN - 1)

        with ExitStack() as ph:
            def sb5(name, shape, dt=fp32):
                return ph.enter_context(nc.sbuf_tensor(name, shape, dt))
            moe_w = sb5("moe_w", [P, 2, TPB, D])
            pos_w = sb5("pos_w5", [P, 2, TPB], u32)
            gp = sb5("gp", [P, 2, TPB * D])
            gt = sb5("gt", [P, 2, TPB * D])
            gg = sb5("gg", [P, TPB * D])
            sg = sb5("sg", [P, TPB * D])
            s_pw = [sem(f"p5_pos_ready_{i}") for i in range(2)]
            s_moe = [sem(f"p5_gathered_{i}") for i in range(2)]
            names = {n: 2 for n in ("gp", "gt", "gg", "sg", "x1")}
            S = {n: sem("p5_" + n) for n in names}

            def at(r, n, c):
                return (r + 1) * names[n] + c

            block = ph.enter_context(nc.Block())

            @block.gpsimd
            def _(pool):
                for n, per in names.items():
                    pool.sem_inc(S[n], per)
                with pool.Fori(0, NB // 2) as r:
                    for i in range(2):
                        pool.wait_ge(S["gp"], at(r, "gp", i + 1 - 2))
                        nc.gpsimd.tensor_copy(pos_w[:, i, :], pos[:, ds((r * 2 + i) * TPB, TPB)]).then_inc(s_pw[i], 1)
                        pool.wait_ge(s_pw[i], r + 1)
                        alone(pool)
                        for j in range(TPB):
                            pool.indirect_dma_start(
                                moe_w[:, i, j, :], None, ys_dram,
                                bass.IndirectOffsetOnAxis(ap=pos_w[:, i, j:j + 1], axis=0)).then_inc(s_moe[i], 16)

            @block.scalar
            def _(act):
                with act.Fori(0, NB // 2) as r:
                    for i in range(2):
                        act.wait_ge(S["gp"], at(r, "gp", i + 1))
                        act.wait_ge(S["gg"], at(r, "gg", i + 1 - 2))
                        nc.scalar.activation(gt[:, i, :], gp[:, i, :], ACT.Tanh, scale=0.5).then_inc(S["gt"], 1)

            @block.vector
            def _(dve):
                with dve.Fori(0, NB // 2) as r:
                    for i in range(2):
                        def rng(a):
                            return a[:, ds((r * 2 + i) * TPB, TPB), :]

                        def tok(a):
                            return a.rearrange("p (j d) -> p j d", d=D)
                        dve.wait_ge(s_moe[i], (r + 1) * 16 * TPB)
                        dve.wait_ge(S["gg"], at(r, "gg", i + 1 - 2))
                        nc.vector.tensor_tensor(tok(gp[:, i, :]), rng(res_all), moe_w[:, i, :, :], ALU.add)\
                            .then_inc(S["gp"], 1)
                        dve.wait_ge(S["gt"], at(r, "gt", i + 1))
                        dve.wait_ge(S["sg"], at(r, "sg", i))
                        nc.vector.scalar_tensor_tensor(gg[:, :], gt[:, i, :], 1.0, gp[:, i, :], ALU.add, ALU.mult)\
                            .then_inc(S["gg"], 1)
                        dve.wait_ge(S["gg"], at(r, "gg", i + 1))
                        dve.wait_ge(S["x1"], at(r, "x1", i))
                        nc.vector.scalar_tensor_tensor(tok(sg[:, :]), tok(gg[:, :]), 0.5, rng(attn_all),
                                                       ALU.mult, ALU.mult).then_inc(S["sg"], 1)
                        dve.wait_ge(S["sg"], at(r, "sg", i + 1))
                        nc.vector.tensor_tensor(rng(x_all), rng(x_all), tok(sg[:, :]), ALU.add).then_inc(S["x1"], 1)
                        dve.wait_ge(S["x1"], at(r, "x1", i + 1))
                        for j in range(TPB):
                            nc.vector.bn_stats(stats[:, ds((r * 2 + i) * TPB + j, 1), :],
                                               x_all[:, ds((r * 2 + i) * TPB + j, 1), :])

        layer0.close()
        with ExitStack() as ph:
            def sb6(name, shape, dt=fp32):
                return ph.enter_context(nc.sbuf_tensor(name, shape, dt))
            NP = NS // 2
            Bbc = vo_all[:, :, :].rearrange("p j d -> p (j d)").rearrange("p (n l) -> p n l", l=L)
            Bbc2 = nf_all[:, :, :].rearrange("p j d -> p (j d)").rearrange("p (n l) -> p n l", l=L)

            def B_pair(q):
                half = Bbc if q < NP // 2 else Bbc2
                m = (2 * q) % NS % (NS // 2)
                return half[:, m:m + 2, :]
            hring = xnT_all[:, :].rearrange("p (r n l) -> p r n l", n=2, l=L)
            dbx = nfT_all[:, :].rearrange("p (r n l) -> p r n l", n=2, l=L)

            W_in = sb6("W_in", [P, DI])
            convw = sb6("convw", [P, KH, TAPS])
            convb = sb6("convb", [P, KH])
            W_x = sb6("W_x", [P, KH, RX])
            W_dt = sb6("W_dt", [P, DI])
            b_dt = sb6("b_dt", [P, KH])
            A = sb6("A", [P, KH, NS])
            Dcol = sb6("Dcol", [P, KH])
            W_out = sb6("W_out", [P, KH, D])
            W_outD = sb6("W_outD", [P, KH, D])
            wi = attn_all[:, :, :].rearrange("p j d -> p (j d)")[:, 0:3 * HID].bitcast(i32)
            wgu = sb6("wgu", [P, 2 * HID])
            wd = sb6("wd", [P, KF, D])
            mean1 = sb6("mean1", [P, NT])
            var1 = sb6("var1", [P, NT])
            tmp1 = sb6("tmp1", [P, NT])
            rs1 = sb6("rs1", [P, NT])
            xn1 = sb6("xn1", [P, TPB, D])
            xn1T = sb6("xn1T", [P, L])
            cbuf = sb6("cbuf", [P, KH, TAPS - 1 + L])
            yh = sb6("yh", [P, KH, L])
            tc_ = sb6("tconv", [P, KH, L])
            xv = sb6("xv", [P, KH, L])
            tf = sb6("tf", [P, L])
            fa = sb6("fa", [P, L])
            hff = sb6("hff", [P, KF, L])
            ssmT = sb6("ssmT", [P, L])
            Cc = sb6("Cc", [P, TPB, RX])
            tg = sb6("tg", [P, L])
            G1 = sb6("G1", [P, L])
            ab = sb6("ab", [P, KH, L])
            rl = sb6("rl", [P, KH, L])
            lg = sb6("lg", [P, KH, L])
            e1 = sb6("e1", [P, KH, L])
            delta = sb6("delta", [P, KH, L])
            du = sb6("du", [P, KH, L])
            acc = sb6("acc", [P, TPB, D])
            ow = sb6("ow", [P, TPB, D])
            og = sb6("og", [P, TPB, D])
            s_lw = sem("p6_weights_loaded")
            s_pad = sem("p6_zeros_set")
            s_st = sem("p6_dve_step")
            s_v1 = sem("p6_var_ready")
            s_r1 = sem("p6_std_ready")
            s_al = sem("p6_A_exp")
            s_set = sem("p6_setup_done")
            s_bst = sem("p6_B_stored")
            s_bld = sem("p6_B_loaded")
            s_o = sem("p6_out_stored")
            names = {"xn": 1, "xT_ps": 1, "xT": 1, "xv0_ps": 1, "xv1_ps": 1, "cb": KH, "tap": KH * (TAPS - 1), "yh": KH,
                     "tc": KH, "xv": KH, "ff_ps": KF, "tf": KF, "fa": KF, "hf": KF, "ssm_ps": 1, "ssm": 1,
                     "C_ps": 1, "C": 1, "dn_ps": 1, "tg": 1, "G1": 1, "dt_ps": KH, "rl": KH, "ey": 1, "lg": 1,
                     "e1": 1, "corr": 1, "sp": 1, "delta": 1, "du": 1, "acc_ps": 1, "acc0": 1,
                     "dA": 2 * NP, "dbx": 2 * NP, "scan": 2 * NP, "G": NS, "acc": NS * TPB, "og": 1, "ow": 1}
            S = {n: sem("p6_" + n) for n in names}

            def at(b, n, c):
                return (b + 1) * names[n] + c

            bA, bB = 6, 7
            dA = [psum[:, 0:2, :], psum[:, 2:4, :]]
            Gb = [4, 5]

            block = ph.enter_context(nc.Block())

            @block.sync
            def _(sp):
                kh = "(h p) a -> p h a"
                loads = [(W_in[:, :], t["W_in"]), (convw[:, :, :], t["conv_w"].rearrange(kh, p=P)),
                         (convb[:, :], t["conv_b"].rearrange("(h p) -> p h", p=P)),
                         (W_x[:, :, :], t["W_x"].rearrange(kh, p=P)),
                         (b_dt[:, :], t["b_dt"].rearrange("(h p) -> p h", p=P)),
                         (A[:, :, :], t["A_log"].rearrange(kh, p=P)),
                         (Dcol[:, :], t["D"].rearrange("(h p) -> p h", p=P)),
                         (W_out[:, :, :], t["W_out"].rearrange(kh, p=P)),
                         (wi[:, 0:HID], t["wg"]), (wi[:, HID:2 * HID], t["wu"]),
                         (wi[:, 2 * HID:3 * HID].rearrange("p (k d) -> p k d", d=D),
                          t["wd"].rearrange("(k p) d -> p k d", p=P))]
                with nc.allow_non_contiguous_dma("columns of small vectors"):
                    for dst, src in loads:
                        sp.dma_start(dst, src).then_inc(s_lw, 16)
                sp.wait_ge(s_pad, 1)
                sp.dma_start(W_dt[0:RDT, :], t["W_dt"]).then_inc(s_lw, 16)
                with sp.Fori(0, NB) as b:
                    sp.wait_ge(S["ssm"], at(b, "ssm", 1))
                    sp.wait_ge(s_bld, (b + 1) * 32)
                    sp.dma_start(bt_dram, ssmT[RDT:RDT + NS, :]).then_inc(s_bst, 16)
                    sp.wait_ge(s_bst, (b + 2) * 16)
                    sp.dma_start(Bbc, bt_dram[None, 0:NS // 2, :].to_broadcast([P, NS // 2, L])).then_inc(s_bld, 16)
                    sp.dma_start(Bbc2, bt_dram[None, NS // 2:NS, :].to_broadcast([P, NS // 2, L])).then_inc(s_bld, 16)
                    sp.wait_ge(S["ow"], at(b, "ow", 1))
                    alone(sp)
                    sp.dma_start(out[ds(b, 1)].rearrange("a (j p) d -> p (a j) d", p=P), ow[:, :, :]).then_inc(s_o, 16)
                sp.wait_ge(s_o, 16 * (NB + 1))

            @block.gpsimd
            def _(pool):
                for n, per in names.items():
                    pool.sem_inc(S[n], per)
                pool.sem_inc(s_bld, 32)
                pool.sem_inc(s_bst, 16)
                pool.sem_inc(s_o, 16)
                with pool.Fori(0, NB) as b:
                    pool.wait_ge(S["du"], at(b, "du", 1))
                    pool.wait_ge(s_bld, (b + 2) * 32)
                    for q in range(NP):
                        for h in range(KH):
                            i = 2 * q + h
                            pool.wait_ge(S["scan"], at(b, "scan", i + 1 - 4))
                            nc.gpsimd.tensor_tensor(dbx[:, i % 4, :, :], B_pair(q),
                                                    du[:, h:h + 1, :].to_broadcast([P, 2, L]), ALU.mult)\
                                .then_inc(S["dbx"], 1)

            @block.tensor
            def _(pe):
                pe.wait_ge(s_set, 1)
                with pe.Fori(0, NB) as b:
                    def w(n, c):
                        pe.wait_ge(S[n], at(b, n, c))

                    def mm(o, l, r, start=True, stop=True):
                        return nc.tensor.matmul(o, l, r, start=start, stop=stop)

                    w("xn", 1)
                    w("delta", 0)
                    w("rl", 0)
                    w("acc0", 0)
                    for j in range(TPB):
                        ins = nc.tensor.transpose(bank[bA][:, j * P:(j + 1) * P], xn1[:, j, :], ident)
                    ins.then_inc(S["xT_ps"], 1)
                    w("xT", 1)
                    mm(bank[bB], W_in[:, 0:P], xn1T[:, :]).then_inc(S["xv0_ps"], 1)
                    mm(bank[bA], W_in[:, P:2 * P], xn1T[:, :]).then_inc(S["xv1_ps"], 1)
                    for k in range(KF):
                        if k == 0:
                            w("cb", 2)
                        else:
                            w("hf", k)
                        mm(bank[bB], wgu[:, k * P:(k + 1) * P], xn1T[:, :])
                        mm(bank[bA], wgu[:, HID + k * P:HID + (k + 1) * P], xn1T[:, :]).then_inc(S["ff_ps"], 1)
                    w("hf", KF)
                    w("xv", KH)
                    for h in range(KH):
                        ins = mm(bank[bA][0:RX, :], W_x[:, h, :], xv[:, h, :], h == 0, h == KH - 1)
                    ins.then_inc(S["ssm_ps"], 1)
                    w("ssm", 1)
                    for j in range(TPB):
                        ins = nc.tensor.transpose(bank[bB][:, j * P:(j + 1) * P], ssmT[:, j * P:(j + 1) * P], ident)
                    ins.then_inc(S["C_ps"], 1)
                    for j in range(TPB):
                        for k in range(KF):
                            ins = mm(bank[bA][:, j * P:(j + 1) * P], hff[:, k, j * P:(j + 1) * P], wd[:, k, :],
                                     k == 0, k == KF - 1)
                    ins.then_inc(S["dn_ps"], 1)
                    w("C", 1)
                    mm(bank[bB], W_dt[:, 0:P], ssmT[:, :]).then_inc(S["dt_ps"], 1)
                    w("G1", 1)
                    mm(bank[bA], W_dt[:, P:2 * P], ssmT[:, :]).then_inc(S["dt_ps"], 1)
                    w("rl", 1)
                    for j in range(TPB):
                        for h in range(KH):
                            ins = mm(bank[bB][:, j * P:(j + 1) * P], xv[:, h, j * P:(j + 1) * P], W_outD[:, h, :],
                                     h == 0, h == KH - 1)
                    ins.then_inc(S["acc_ps"], 1)
                    for n in range(NS):
                        q = n // 2
                        w("scan", 2 * q + 2)
                        w("acc", (n + 1 - 2) * TPB)
                        for j in range(TPB):
                            for h in range(KH):
                                ins = mm(bank[Gb[n % 2]][:, j * P:(j + 1) * P],
                                         hring[:, (2 * q + h) % 4, n % 2, j * P:(j + 1) * P], W_out[:, h, :],
                                         h == 0, h == KH - 1)
                        ins.then_inc(S["G"], 1)

            @block.scalar
            def _(act):
                act.wait_ge(s_v1, 1)
                nc.scalar.activation(tmp1[:, :], var1[:, :], ACT.Sqrt).then_inc(s_r1, 1)
                act.wait_ge(s_v1, 2)
                nc.scalar.activation(A[:, :, :], A[:, :, :], ACT.Exp).then_inc(s_al, 1)
                act.wait_ge(s_set, 1)
                with act.Fori(0, NB) as b:
                    def w(n, c):
                        act.wait_ge(S[n], at(b, n, c))

                    w("xT_ps", 1)
                    w("ff_ps", 0)
                    nc.scalar.activation(xn1T[:, :], bank[bA], ACT.Copy).then_inc(S["xT"], 1)
                    for h, (n, bk) in enumerate((("xv0_ps", bB), ("xv1_ps", bA))):
                        w(n, 1)
                        w("yh", h + 1 - KH)
                        nc.scalar.activation(cbuf[:, h, TAPS - 1:TAPS - 1 + L], bank[bk], ACT.Copy).then_inc(S["cb"], 1)
                    for k in range(KF):
                        w("ff_ps", k + 1)
                        w("fa", k)
                        nc.scalar.activation(tf[:, :], bank[bB], ACT.Tanh, scale=0.5).then_inc(S["tf"], 1)
                    for h in range(KH):
                        w("yh", h + 1)
                        w("xv", h + 1 - KH)
                        nc.scalar.activation(tc_[:, h, :], yh[:, h, :], ACT.Tanh).then_inc(S["tc"], 1)
                    w("ssm_ps", 1)
                    w("dt_ps", 0)
                    act.wait_ge(s_bst, (b + 1) * 16)
                    nc.scalar.activation(ssmT[0:RX, :], bank[bA][0:RX, :], ACT.Copy).then_inc(S["ssm"], 1)
                    w("dn_ps", 1)
                    w("G1", 0)
                    nc.scalar.activation(tg[:, :], bank[bA], ACT.Tanh, scale=0.5).then_inc(S["tg"], 1)
                    w("corr", 0)
                    w("lg", 0)
                    w("sp", 0)
                    w("delta", 0)
                    for h, bk in enumerate((bB, bA)):
                        w("dt_ps", h + 1)
                        nc.scalar.activation(ab[:, h, :], bank[bk], ACT.Abs, bias=b_dt[:, h:h + 1])
                        nc.scalar.activation(rl[:, h, :], bank[bk], ACT.Relu, bias=b_dt[:, h:h + 1]).then_inc(S["rl"], 1)
                    w("rl", KH)
                    nc.scalar.activation(ab[:, :, :], ab[:, :, :], ACT.Exp, scale=-1.0).then_inc(S["ey"], 1)
                    w("ey", 1)
                    nc.scalar.activation(lg[:, :, :], ab[:, :, :], ACT.Ln, bias=1.0).then_inc(S["lg"], 1)
                    w("delta", 1)
                    for q in range(NP):
                        for h in range(KH):
                            i = 2 * q + h
                            w("scan", i + 1 - 2)
                            for k in range(2):
                                ins = nc.scalar.activation(dA[i % 2][:, k, 1:L], delta[:, h, 1:L], ACT.Exp,
                                                           scale=A[:, h, 2 * q + k:2 * q + k + 1])
                            ins.then_inc(S["dA"], 1)

            @block.vector
            def _(dve):
                n = [0]

                def link(ins):
                    n[0] += 1
                    ins.then_inc(s_st, 1)
                    dve.wait_ge(s_st, n[0])

                nc.vector.memset(ssmT[:, :], 0.0)
                nc.vector.memset(W_dt[:, :], 0.0).then_inc(s_pad, 1)
                nc.vector.memset(cbuf[:, :, 0:TAPS - 1], 0.0)
                for d in dA:
                    nc.vector.memset(d[:, :, 0:1], 0.0)
                mean_var(dve, link, mean1[:, :], var1[:, :], tmp1[:, :], stats)
                link(nc.vector.tensor_scalar(var1[:, :], var1[:, :], LN_EPS, None, ALU.add))
                dve.sem_inc(s_v1, 1)
                dve.wait_ge(s_r1, 1)
                link(nc.vector.reciprocal(rs1[:, :], tmp1[:, :]))
                dve.wait_ge(s_lw, 16 * 12)
                link(nc.vector.tensor_scalar(A[:, :, :], A[:, :, :], A_LOG_MAX, None, ALU.min))
                dve.sem_inc(s_v1, 1)
                dve.wait_ge(s_al, 1)
                nc.vector.tensor_scalar(A[:, :, :], A[:, :, :], -1.0, None, ALU.mult)
                nc.vector.tensor_scalar(convw[:, :, :], convw[:, :, :], 0.5, None, ALU.mult)
                nc.vector.tensor_scalar(convb[:, :], convb[:, :], 0.5, None, ALU.mult)
                for h in range(KH):
                    nc.vector.tensor_scalar(W_outD[:, h, :], W_out[:, h, :], Dcol[:, h:h + 1], None, ALU.mult)
                nc.vector.tensor_scalar(wgu[:, :], wi[:, 0:2 * HID], DEQUANT, None, ALU.mult)
                link(nc.vector.tensor_scalar(wd[:, :, :].rearrange("p k d -> p (k d)"), wi[:, 2 * HID:3 * HID],
                                             DEQUANT, None, ALU.mult))
                dve.sem_inc(s_set, 1)
                with dve.Fori(0, NB) as b:
                    def w(n, c):
                        dve.wait_ge(S[n], at(b, n, c))

                    w("xT_ps", 0)
                    for j in range(TPB):
                        ins = nc.vector.tensor_scalar(xn1[:, j, :], x_all[:, ds(b * TPB + j, 1), :],
                                                      mean1[:, ds(b * TPB + j, 1)], rs1[:, ds(b * TPB + j, 1)],
                                                      ALU.subtract, ALU.mult)
                    ins.then_inc(S["xn"], 1)
                    for h in range(KH):
                        w("cb", h + 1)
                        w("tc", h + 1 - KH)
                        w("xv", h + 1 - KH)
                        nc.vector.tensor_scalar(yh[:, h, :], cbuf[:, h, 0:L], convw[:, h, 0:1], convb[:, h:h + 1],
                                                ALU.mult, ALU.add).then_inc(S["tap"], 1)
                        for k in range(1, TAPS):
                            w("tap", h * (TAPS - 1) + k)
                            ins = nc.vector.scalar_tensor_tensor(yh[:, h, :], cbuf[:, h, k:k + L],
                                                                 convw[:, h, k:k + 1], yh[:, h, :],
                                                                 ALU.mult, ALU.add)
                            ins.then_inc(S["tap" if k < TAPS - 1 else "yh"], 1)
                    for k in range(KF):
                        w("tf", k + 1)
                        w("hf", k)
                        nc.vector.scalar_tensor_tensor(fa[:, :], tf[:, :], 1.0, bank[bB], ALU.add, ALU.mult)\
                            .then_inc(S["fa"], 1)
                        w("fa", k + 1)
                        w("dn_ps", 0)
                        nc.vector.scalar_tensor_tensor(hff[:, k, :], fa[:, :], 0.5, bank[bA], ALU.mult, ALU.mult)\
                            .then_inc(S["hf"], 1)
                    w("acc_ps", 0)
                    w("du", 0)
                    for h in range(KH):
                        w("tc", h + 1)
                        nc.vector.scalar_tensor_tensor(xv[:, h, :], tc_[:, h, :], 1.0, yh[:, h, :],
                                                       ALU.add, ALU.mult).then_inc(S["xv"], 1)
                    w("C_ps", 1)
                    w("acc", 0)
                    nc.vector.tensor_copy(Cc[:, :, :], bank[bB].rearrange("p (j r) -> p j r", r=P)[:, :, 0:RX])\
                        .then_inc(S["C"], 1)
                    w("tg", 1)
                    w("og", 0)
                    nc.vector.scalar_tensor_tensor(G1[:, :], tg[:, :], 1.0, bank[bA], ALU.add, ALU.mult)\
                        .then_inc(S["G1"], 1)
                    w("ey", 1)
                    w("delta", 0)
                    nc.vector.tensor_scalar(e1[:, :, :], ab[:, :, :], 1.0, 1.0, ALU.add, ALU.subtract).then_inc(S["e1"], 1)
                    w("e1", 1)
                    nc.vector.tensor_tensor(e1[:, :, :], ab[:, :, :], e1[:, :, :], ALU.subtract).then_inc(S["corr"], 1)
                    w("corr", 1)
                    w("lg", 1)
                    nc.vector.tensor_tensor(e1[:, :, :], e1[:, :, :], lg[:, :, :], ALU.add).then_inc(S["sp"], 1)
                    w("sp", 1)
                    w("rl", KH)
                    w("dA", 0)
                    w("du", 0)
                    nc.vector.tensor_tensor(delta[:, :, :], e1[:, :, :], rl[:, :, :], ALU.add).then_inc(S["delta"], 1)
                    w("delta", 1)
                    w("dbx", 0)
                    nc.vector.tensor_tensor(du[:, :, :], delta[:, :, :], xv[:, :, :], ALU.mult).then_inc(S["du"], 1)
                    w("acc_ps", 1)
                    nc.vector.tensor_copy(acc[:, :, :], bank[bB].rearrange("p (j d) -> p j d", d=D))\
                        .then_inc(S["acc0"], 1)
                    w("acc0", 1)

                    def scan(q, h):
                        i = 2 * q + h
                        w("dA", i + 1)
                        w("dbx", i + 1)
                        w("G", 2 * (q + 1 - 2))
                        nc.vector.tensor_tensor_scan(hring[:, i % 4, :, :].rearrange("p n l -> p (n l)"),
                                                     dA[i % 2].rearrange("p n l -> p (n l)"),
                                                     dbx[:, i % 4, :, :].rearrange("p n l -> p (n l)"),
                                                     0.0, ALU.mult, ALU.add).then_inc(S["scan"], 1)

                    def add_state(m):
                        w("G", m + 1)
                        for j in range(TPB):
                            if m:
                                w("acc", (m - 1) * TPB + j + 1)
                            nc.vector.scalar_tensor_tensor(acc[:, j, :], bank[Gb[m % 2]][:, j * P:(j + 1) * P],
                                                           Cc[:, j, RDT + NS + m:RDT + NS + m + 1], acc[:, j, :],
                                                           ALU.mult, ALU.add).then_inc(S["acc"], 1)

                    for q in range(NP):
                        scan(q, 0)
                        scan(q, 1)
                        if q:
                            add_state(2 * q - 2)
                            add_state(2 * q - 1)
                    add_state(NS - 2)
                    add_state(NS - 1)
                    w("acc", NS * TPB)
                    w("ow", 0)
                    nc.vector.scalar_tensor_tensor(og[:, :, :], acc[:, :, :], 0.5,
                                                   G1[:, :].rearrange("p (j d) -> p j d", d=D),
                                                   ALU.mult, ALU.mult).then_inc(S["og"], 1)
                    w("og", 1)
                    w("ow", 0)
                    dve.wait_ge(s_o, (b + 1) * 16)
                    nc.vector.tensor_tensor(ow[:, :, :], og[:, :, :], x_all[:, ds(b * TPB, TPB), :], ALU.add)\
                        .then_inc(S["ow"], 1)


_RENAME = {"x": "L0_attn_x", "Wv": "L0_attn_Wv", "bq": "L0_attn_bq", "bk": "L0_attn_bk", "bv": "L0_attn_bv",
           "bo": "L0_attn_bo", "ln_w": "L0_ffn_ln_w", "ln_b": "L0_ffn_ln_b", "router": "L0_ffn_router_w",
           "gate": "L0_ffn_gate_w", "up": "L0_ffn_up_w", "down": "L0_ffn_down_w", "sh_gate": "L0_ffn_sh_gate",
           "sh_up": "L0_ffn_sh_up", "sh_down": "L0_ffn_sh_down", "W_in": "L1_attn_W_in", "conv_b": "L1_attn_conv_b",
           "W_x": "L1_attn_W_x", "W_dt": "L1_attn_W_dt", "b_dt": "L1_attn_b_dt", "A_log": "L1_attn_A_log",
           "D": "L1_attn_D", "W_out": "L1_attn_W_out"}
_TRANSPOSED = {"WqT": "L0_attn_Wq", "WkT": "L0_attn_Wk", "WoT": "L0_attn_Wo", "wg": "L1_ffn_w_gate",
               "wu": "L1_ffn_w_up", "wd": "L1_ffn_w_down"}


def _shape_constants(tiles, experts):
    import numpy as np
    p = np.arange(128)
    over = np.ones((128, 1), np.float32)
    parts = [np.eye(128), (p[:, None] < p[None, :]), np.ones((128, 128)), over * (128 * np.arange(tiles)),
             over * np.arange(tiles + experts), over * (np.arange(experts) - experts)]
    return np.ascontiguousarray(np.concatenate([a.astype(np.float32) for a in parts], axis=1))


def kernel(**inputs):
    import numpy as _np
    import concourse.bacc as _bacc
    from concourse import mybir as _mybir
    from concourse.bass_utils import run_bass_kernel_spmd as _run

    arrays = {n: _np.ascontiguousarray(inputs[m]) for n, m in _RENAME.items()}
    arrays |= {n: _np.ascontiguousarray(_np.asarray(inputs[m]).T) for n, m in _TRANSPOSED.items()}
    arrays["conv_w"] = _np.ascontiguousarray(_np.asarray(inputs["L1_attn_conv_w"])[:, 0, :])
    nb, length, d = arrays["x"].shape
    arrays["const"] = _shape_constants(nb * length // 128, arrays["router"].shape[1])
    nc = _bacc.Bacc("TRN2", target_bir_lowering=False, num_devices=1)
    t = {n: nc.dram_tensor(f"in_{n}_dram", a.shape, _mybir.dt.from_np(a.dtype), kind="ExternalInput").ap()
         for n, a in arrays.items()}
    out = nc.dram_tensor("out_dram", (nb, length, d), _mybir.dt.float32, kind="ExternalOutput").ap()
    attention_moe_mamba_ffn(nc, t, out)
    r = _run(nc, [{f"in_{n}_dram": a for n, a in arrays.items()}], core_ids=[0])
    return r.results[0]["out_dram"]
```

```python
import concourse.bass as bass
from concourse import mybir
from contextlib import ExitStack


def attention_moe_mamba_ffn(nc, t, out):
    fp32 = mybir.dt.float32
    i32 = mybir.dt.int32
    u32 = mybir.dt.uint32
    ALU = mybir.AluOpType
    ACT = mybir.ActivationFunctionType
    X = mybir.AxisListType.X
    ds = bass.ds

    P = 128
    NB, L, D = t["x"].shape
    TPB = L // P
    NT = NB * TPB
    NE = t["router"].shape[1]
    I = t["gate"].shape[2]
    KI = I // P
    SLOT_TILES = NT + NE
    LN_EPS = 1e-5
    DI = t["W_in"].shape[1]
    KH = DI // P
    NS = t["A_log"].shape[1]
    TAPS = t["conv_w"].shape[1]
    RX = t["W_x"].shape[1]
    RDT = RX - 2 * NS
    HID = t["wg"].shape[1]
    KF = HID // P
    DEQUANT = 1.0 / 127.0
    A_LOG_MAX = 80.0

    ctx = ExitStack()
    with ctx:
        def sb(name, shape, dt=fp32):
            return ctx.enter_context(nc.sbuf_tensor(name, shape, dt))

        def sem(name):
            return ctx.enter_context(nc.semaphore(name))

        xs_dram = nc.dram_tensor("xs_dram", [SLOT_TILES * P, D], fp32, kind="Internal").ap()
        ys_dram = nc.dram_tensor("ys_dram", [SLOT_TILES * P, D], fp32, kind="Internal").ap()
        bt_dram = nc.dram_tensor("bt_dram", [NB, NS, L], fp32, kind="Internal").ap()

        x_all = sb("x_all", [P, NT, D])
        res_all = sb("res_all", [P, NT, D])
        xnT_all = sb("xnT_all", [P, NB * L])
        nfT_all = sb("nfT_all", [P, NB * L])
        nf_all = sb("nf_all", [P, NT, D])
        vo_all = sb("vo_all", [P, NT, D])
        attn_all = sb("attn_all", [P, NT, D])
        const = sb("const", [P, t["const"].shape[1]])
        psum = ctx.enter_context(nc.psum_tensor("psum", [P, 8, 512], fp32))
        stats = sb("stats", [P, NT, 6])
        W_in = sb("W_in", [P, DI])
        convw = sb("convw", [P, KH, TAPS])
        convb = sb("convb", [P, KH])
        W_x = sb("W_x", [P, KH, RX])
        W_dt = sb("W_dt", [P, DI])
        b_dt = sb("b_dt", [P, KH])
        A = sb("A", [P, KH, NS])
        Dcol = sb("Dcol", [P, KH])
        W_out = sb("W_out", [P, KH, D])
        W_outD = sb("W_outD", [P, KH, D])
        wgu = sb("wgu", [P, 2 * HID])
        wd = sb("wd", [P, KF, D])
        wi = nf_all[:, :, :].rearrange("p j d -> p (j d)")[:, 0:3 * HID].bitcast(i32)
        xn1T_all = vo_all[:, :, :].rearrange("p j d -> p (j d)")
        layer0 = ctx.enter_context(ExitStack())

        def sb(name, shape, dt=fp32):
            return layer0.enter_context(nc.sbuf_tensor(name, shape, dt))

        gu = sb("gu", [P, NE, 2 * I])
        down = sb("down", [P, NE, KI, D])
        shgu = sb("shgu", [P, 2 * I])
        shdown = sb("shdown", [P, KI, D])
        WqT = sb("WqT", [P, D])
        WkT = sb("WkT", [P, D])
        Wv = sb("Wv", [P, D])
        WoT = sb("WoT", [P, D])
        Wvo = sb("Wvo", [P, D])
        vobias = sb("vobias", [P, D])
        cols = sb("cols", [P, 5])
        rows = sb("rows", [P, 3, D])
        router = sb("router", [P, NE])
        ident = const[:, 0:P]
        lower = const[:, P:2 * P]
        ones = const[:, 2 * P:3 * P]
        thr = const[:, 3 * P:3 * P + NT]
        slot_tile = const[:, 3 * P + NT:3 * P + NT + SLOT_TILES]
        eidx = const[:, 3 * P + NT + SLOT_TILES:3 * P + NT + SLOT_TILES + NE]
        bank = [psum[:, i, :] for i in range(8)]

        s_passed = sem("waits_passed")

        def alone(eng):
            eng.sem_inc(s_passed, 1)

        s_w = sem("weights_loaded")
        s_we = sem("attention_and_expert_weights_loaded")
        s_lw = sem("layer1_weights_loaded")
        s_x = [sem(f"x_loaded_{i}") for i in range(NB)]

        mean_r = sb("mean_r", [P, NT])
        rstd1 = sb("rstd1", [P, NT])
        rstd12 = sb("rstd12", [P, NT])
        score = sb("score", [P, NT])
        pos = sb("pos", [P, NT], u32)
        logits = sb("logits", [P, NT, NE])
        guoff = sb("guoff", [P, SLOT_TILES], i32)

        def mean_var(dve, link, mean, var, tmp, st):
            me, mo = st[:, :, 1], st[:, :, 4]
            link(nc.vector.tensor_tensor(mean, me, mo, ALU.add))
            link(nc.vector.tensor_scalar(mean, mean, 0.5, None, ALU.mult))
            link(nc.vector.tensor_tensor(tmp, me, mo, ALU.subtract))
            link(nc.vector.tensor_tensor(tmp, tmp, tmp, ALU.mult))
            link(nc.vector.tensor_tensor(var, st[:, :, 2], st[:, :, 5], ALU.add))
            link(nc.vector.tensor_scalar(var, var, 1.0 / D, None, ALU.mult))
            link(nc.vector.scalar_tensor_tensor(var, tmp, 0.25, var, ALU.mult, ALU.add))

        with ExitStack() as ph:
            def sb1(name, shape, dt=fp32):
                return ph.enter_context(nc.sbuf_tensor(name, shape, dt))
            var = sb1("var", [P, NT])
            tmp = sb1("tmp", [P, NT])
            std = sb1("std", [P, NT])
            xn_w = sb1("xn_w", [P, TPB, D])
            z_w = sb1("z_w", [P, TPB, D])
            zw_w = sb1("zw_w", [P, TPB, D])
            xnT_w = sb1("xnT_w", [P, L])
            nfT_w = sb1("nfT_w", [P, L])
            zeros = sb1("zeros", [P, SLOT_TILES * D // 4])
            bvb = sb1("bvb", [P, P])
            names = {"xn_done": 1, "z_done": 1, "xT_ps": 1, "zT_ps": 1, "xnT_w_done": 1, "nfT_w_done": 1,
                     "vo_ps": 1, "logit_ps": 1, "vo_done": 1, "logit_done": 1, "xnT_copied": 1,
                     "xn_copied": 1, "nfT_copied": 1, "zw": 1, "nf": 1}
            S = {n: sem("p1_" + n) for n in names}
            s_dve = sem("p1_dve_step")
            s_var = sem("p1_var_ready")
            s_std = sem("p1_std_ready")
            s_zero = sem("p1_zeros_ready")
            s_zd = sem("p1_slots_zeroed")
            s_bvb = sem("p1_bv_broadcast")
            s_wvo = sem("p1_wvo_ps")
            s_wvo_sb = sem("p1_wvo_sb")

            def at(b, n, c=1):
                return (b + 1) * names[n] + c

            block = ph.enter_context(nc.Block())

            @block.sync
            def _(sp):
                for b in range(NB):
                    sp.dma_start(x_all[:, b * TPB:(b + 1) * TPB, :],
                                 t["x"][b].rearrange("(j p) d -> p j d", p=P)).then_inc(s_x[b], 16)
                sp.wait_ge(s_w, 16 * 12)
                for dst, src in [(WqT[:, :], t["WqT"]), (WkT[:, :], t["WkT"]),
                                 (shgu[:, 0:I], t["sh_gate"]), (shgu[:, I:2 * I], t["sh_up"]),
                                 (shdown[:, :, :], t["sh_down"].rearrange("(k p) h -> p k h", p=P)),
                                 (gu[:, :, 0:I], t["gate"].rearrange("e h i -> h e i")),
                                 (gu[:, :, I:2 * I], t["up"].rearrange("e h i -> h e i")),
                                 (down[:, :, :, :], t["down"].rearrange("e (k p) h -> p e k h", p=P))]:
                    sp.dma_start(dst, src).then_inc(s_we, 16)
                sp.wait_ge(s_zero, 1)
                z4 = xs_dram.rearrange("(a p r) d -> a p (r d)", a=4, p=P)
                for a in range(4):
                    sp.dma_start(z4[a], zeros[:, :]).then_inc(s_zd, 16)
                sp.wait_ge(s_zd, 64)

            @block.scalar
            def _(act):
                loads = [(const[:, :], t["const"]), (Wv[:, :], t["Wv"]), (WoT[:, :], t["WoT"]),
                         (router[:, :], t["router"])]
                loads += [(cols[:, i:i + 1], t[n].rearrange("(p a) -> p a", a=1))
                          for i, n in enumerate(("bq", "bk", "ln_w", "ln_b", "bv"))]
                loads += [(rows[:, i, :], t[n].rearrange("(a d) -> a d", a=1).to_broadcast([P, D]))
                          for i, n in enumerate(("bo", "ln_w", "ln_b"))]
                for dst, src in loads:
                    act.dma_start(dst, src).then_inc(s_w, 16)
                act.wait_ge(s_var, 1)
                nc.scalar.activation(std[:, :], var[:, :], ACT.Sqrt).then_inc(s_std, 1)
                act.wait_ge(s_var, 2)
                nc.scalar.activation(tmp[:, :], var[:, :], ACT.Sqrt).then_inc(s_std, 1)
                act.wait_ge(s_w, 16 * 12)
                with act.Fori(0, NB) as b:
                    act.wait_ge(S["xT_ps"], at(b, "xT_ps"))
                    act.wait_ge(S["vo_ps"], at(b, "vo_ps", 0))
                    act.wait_ge(S["xnT_copied"], at(b, "xnT_copied", 0))
                    nc.scalar.activation(xnT_w[:, :], bank[0], ACT.Copy).then_inc(S["xnT_w_done"], 1)
                    act.wait_ge(S["zT_ps"], at(b, "zT_ps"))
                    act.wait_ge(S["logit_ps"], at(b, "logit_ps", 0))
                    act.wait_ge(S["nfT_copied"], at(b, "nfT_copied", 0))
                    nc.scalar.activation(nfT_w[:, :], bank[1], ACT.Identity, bias=cols[:, 3:4],
                                         scale=cols[:, 2:3]).then_inc(S["nfT_w_done"], 1)
                    act.wait_ge(S["nfT_w_done"], at(b, "nfT_w_done"))
                    nc.scalar.activation(nfT_all[:, ds(b * L, L)], nfT_w[:, :], ACT.Copy).then_inc(S["nfT_copied"], 1)

            @block.gpsimd
            def _(pool):
                nc.gpsimd.memset(zeros[:, :], 0.0).then_inc(s_zero, 1)
                nc.gpsimd.memset(W_dt[:, :], 0.0)
                for n, per in names.items():
                    pool.sem_inc(S[n], per)
                with pool.Fori(0, NB) as b:
                    pool.wait_ge(S["xn_done"], at(b, "xn_done"))
                    nc.gpsimd.tensor_copy(res_all[:, ds(b * TPB, TPB), :], xn_w[:, :, :]).then_inc(S["xn_copied"], 1)
                    pool.wait_ge(S["xnT_w_done"], at(b, "xnT_w_done"))
                    nc.gpsimd.tensor_copy(xnT_all[:, ds(b * L, L)], xnT_w[:, :]).then_inc(S["xnT_copied"], 1)

            @block.tensor
            def _(pe):
                pe.wait_ge(s_w, 16 * 12)
                nc.tensor.matmul(bank[4][:, 0:D], Wv[:, :], WoT[:, :], start=True, stop=True)
                pe.wait_ge(s_bvb, 1)
                nc.tensor.matmul(bank[4][:, D:2 * D], bvb[:, :], WoT[:, :], start=True, stop=True).then_inc(s_wvo, 1)
                pe.wait_ge(s_wvo_sb, 1)
                with pe.Fori(0, NB) as b:
                    pe.wait_ge(S["xn_done"], at(b, "xn_done"))
                    pe.wait_ge(S["xnT_w_done"], at(b, "xnT_w_done", 0))
                    for j in range(TPB):
                        ins = nc.tensor.transpose(bank[0][:, j * P:(j + 1) * P], xn_w[:, j, :], ident)
                    ins.then_inc(S["xT_ps"], 1)
                    pe.wait_ge(S["z_done"], at(b, "z_done"))
                    pe.wait_ge(S["nfT_w_done"], at(b, "nfT_w_done", 0))
                    for j in range(TPB):
                        ins = nc.tensor.transpose(bank[1][:, j * P:(j + 1) * P], z_w[:, j, :], ident)
                    ins.then_inc(S["zT_ps"], 1)
                    pe.wait_ge(S["xnT_w_done"], at(b, "xnT_w_done"))
                    pe.wait_ge(S["vo_done"], at(b, "vo_done", 0))
                    for j in range(TPB):
                        ins = nc.tensor.matmul(bank[2][:, j * P:(j + 1) * P], xnT_w[:, j * P:(j + 1) * P], Wvo[:, :],
                                               start=True, stop=True)
                    ins.then_inc(S["vo_ps"], 1)
                    pe.wait_ge(S["nfT_w_done"], at(b, "nfT_w_done"))
                    pe.wait_ge(S["logit_done"], at(b, "logit_done", 0))
                    for j in range(TPB):
                        ins = nc.tensor.matmul(bank[3][:, j * NE:(j + 1) * NE], nfT_w[:, j * P:(j + 1) * P],
                                               router[:, :], start=True, stop=True)
                    ins.then_inc(S["logit_ps"], 1)

            @block.vector
            def _(dve):
                n = [0]

                def link(ins):
                    n[0] += 1
                    ins.then_inc(s_dve, 1)
                    dve.wait_ge(s_dve, n[0])

                for b in range(NB):
                    dve.wait_ge(s_x[b], 16)
                    for j in range(TPB):
                        ins = nc.vector.bn_stats(stats[:, b * TPB + j, :], x_all[:, b * TPB + j, :])
                link(ins)
                mean_var(dve, link, mean_r[:, :], var[:, :], tmp[:, :], stats)
                nc.vector.tensor_copy(rstd12[:, :], var[:, :])
                link(nc.vector.tensor_scalar(std[:, :], var[:, :], 1.0, None, ALU.mult))
                link(nc.vector.tensor_scalar(var[:, :], var[:, :], LN_EPS, None, ALU.add))
                nc.vector.tensor_copy(rstd1[:, :], var[:, :]).then_inc(s_var, 1)
                dve.wait_ge(s_std, 1)
                link(nc.vector.reciprocal(rstd1[:, :], std[:, :]))
                link(nc.vector.tensor_tensor(var[:, :], rstd1[:, :], rstd1[:, :], ALU.mult))
                link(nc.vector.tensor_tensor(var[:, :], var[:, :], rstd12[:, :], ALU.mult))
                nc.vector.tensor_scalar(var[:, :], var[:, :], LN_EPS, None, ALU.add).then_inc(s_var, 1)
                dve.wait_ge(s_std, 2)
                link(nc.vector.reciprocal(tmp[:, :], tmp[:, :]))
                link(nc.vector.tensor_tensor(rstd12[:, :], tmp[:, :], rstd1[:, :], ALU.mult))
                dve.wait_ge(s_w, 16 * 12)
                link(nc.vector.memset(bvb[:, :], 1.0))
                nc.vector.tensor_scalar(bvb[:, :], bvb[:, :], cols[:, 4:5], None, ALU.mult).then_inc(s_bvb, 1)
                dve.wait_ge(s_wvo, 1)
                nc.vector.tensor_copy(Wvo[:, :], bank[4][:, 0:D])
                link(nc.vector.tensor_tensor(vobias[:, :], bank[4][:, D:2 * D], rows[:, 0, :], ALU.add))
                dve.sem_inc(s_wvo_sb, 1)
                def norms(b):
                    dve.wait_ge(S["xT_ps"], at(b, "xT_ps", 0))
                    dve.wait_ge(S["xn_copied"], at(b, "xn_copied", 0))
                    for j in range(TPB):
                        ins = nc.vector.tensor_scalar(xn_w[:, j, :], x_all[:, ds(b * TPB + j, 1), :],
                                                      mean_r[:, ds(b * TPB + j, 1)], rstd1[:, ds(b * TPB + j, 1)],
                                                      ALU.subtract, ALU.mult)
                    ins.then_inc(S["xn_done"], 1)
                    dve.wait_ge(S["zT_ps"], at(b, "zT_ps", 0))
                    dve.wait_ge(S["zw"], at(b, "zw", 0))
                    for j in range(TPB):
                        ins = nc.vector.tensor_scalar(z_w[:, j, :], x_all[:, ds(b * TPB + j, 1), :],
                                                      mean_r[:, ds(b * TPB + j, 1)], rstd12[:, ds(b * TPB + j, 1)],
                                                      ALU.subtract, ALU.mult)
                    ins.then_inc(S["z_done"], 1)
                    dve.wait_ge(S["z_done"], at(b, "z_done"))
                    dve.wait_ge(S["nf"], at(b, "nf", 0))
                    nc.vector.tensor_tensor(zw_w[:, :, :], z_w[:, :, :], rows[:, 1:2, :].to_broadcast([P, TPB, D]),
                                            ALU.mult).then_inc(S["zw"], 1)
                    dve.wait_ge(S["zw"], at(b, "zw"))
                    nc.vector.tensor_tensor(nf_all[:, ds(b * TPB, TPB), :], zw_w[:, :, :],
                                            rows[:, 2:3, :].to_broadcast([P, TPB, D]), ALU.add).then_inc(S["nf"], 1)

                def values_logits(b):
                    dve.wait_ge(S["vo_ps"], at(b, "vo_ps"))
                    nc.vector.tensor_tensor(vo_all[:, ds(b * TPB, TPB), :],
                                            bank[2].rearrange("p (j d) -> p j d", d=D),
                                            vobias[:, None, :].to_broadcast([P, TPB, D]), ALU.add)\
                        .then_inc(S["vo_done"], 1)
                    dve.wait_ge(S["logit_ps"], at(b, "logit_ps"))
                    nc.vector.tensor_copy(logits[:, ds(b * TPB, TPB), :],
                                          bank[3][:, 0:TPB * NE].rearrange("p (j e) -> p j e", e=NE))\
                        .then_inc(S["logit_done"], 1)

                norms(0)
                with dve.Fori(1, NB) as b:
                    norms(b)
                    values_logits(b - 1)
                values_logits(NB - 1)

        with ExitStack() as ph:
            def sb2(name, shape, dt=fp32):
                return ph.enter_context(nc.sbuf_tensor(name, shape, dt))
            top = sb2("top", [P, NT])
            eq = sb2("eq", [P, NT, NE])
            first = sb2("first", [P, NT])
            onehot = sb2("onehot", [P, NE, NT])
            cnt = sb2("cnt", [P, NE, NT])
            cum = sb2("cum", [P, NE, NT])
            big = sb2("big", [P, SLOT_TILES, NE])
            tot = sb2("tot", [P, NE])
            ntile = sb2("ntile", [P, NE])
            tend = sb2("tend", [P, NE])
            base = sb2("base", [P, NE])
            slot = sb2("slot", [P, NE, NT])
            posf = sb2("posf", [P, NT])
            exf = sb2("exf", [P, SLOT_TILES])
            s_oh = sem("p2_onehot_ready")
            s_cnt = sem("p2_counts_ps")
            s_top = sem("p2_top_ready")
            s_tanh = sem("p2_tanh_ready")
            s_dve2 = sem("p2_dve_step")
            block = ph.enter_context(nc.Block())

            @block.tensor
            def _(pe):
                pe.wait_ge(s_oh, 1)
                oh = onehot[:, :, :].rearrange("p e j -> p (e j)")
                nc.tensor.matmul(bank[0][:, 0:NE * NT], ones, oh, start=True, stop=True)
                nc.tensor.matmul(bank[1][:, 0:NE * NT], lower, oh, start=True, stop=True).then_inc(s_cnt, 1)

            @block.scalar
            def _(act):
                act.wait_ge(s_top, 1)
                nc.scalar.activation(score[:, :], top[:, :], ACT.Tanh, scale=0.5).then_inc(s_tanh, 1)

            @block.vector
            def _(dve):
                n = [0]

                def link(ins):
                    n[0] += 1
                    ins.then_inc(s_dve2, 1)
                    dve.wait_ge(s_dve2, n[0])

                link(nc.vector.tensor_reduce(top[:, :], logits[:, :, :], X, ALU.max))
                link(nc.vector.tensor_tensor(eq[:, :, :], logits[:, :, :],
                                             top[:, :, None].to_broadcast([P, NT, NE]), ALU.is_equal))
                dve.sem_inc(s_top, 1)
                link(nc.vector.tensor_tensor(eq[:, :, :], eq[:, :, :],
                                             eidx[:, None, :].to_broadcast([P, NT, NE]), ALU.mult))
                link(nc.vector.tensor_reduce(first[:, :], eq[:, :, :], X, ALU.min))
                link(nc.vector.tensor_tensor(onehot[:, :, :], first[:, None, :].to_broadcast([P, NE, NT]),
                                             eidx[:, :, None].to_broadcast([P, NE, NT]), ALU.is_equal))
                dve.sem_inc(s_oh, 1)
                dve.wait_ge(s_tanh, 1)
                nc.vector.tensor_scalar(score[:, :], score[:, :], 0.5, 0.5, ALU.mult, ALU.add)
                dve.wait_ge(s_cnt, 1)
                link(nc.vector.tensor_copy(cnt[:, :, :], bank[0][:, 0:NE * NT].rearrange("p (e j) -> p e j", e=NE)))
                link(nc.vector.tensor_reduce(tot[:, :], cnt[:, :, :], X, ALU.add))
                link(nc.vector.tensor_tensor_scan(cum[:, :, :].rearrange("p e j -> p (e j)"),
                                                  cnt[:, :, :].rearrange("p e j -> p (e j)"),
                                                  cnt[:, :, :].rearrange("p e j -> p (e j)"),
                                                  0.0, ALU.add, ALU.bypass))
                link(nc.vector.tensor_tensor(slot[:, :, :], tot[:, :, None].to_broadcast([P, NE, NT]),
                                             thr[:, None, :].to_broadcast([P, NE, NT]), ALU.is_gt))
                link(nc.vector.tensor_reduce(ntile[:, :], slot[:, :, :], X, ALU.add))
                link(nc.vector.tensor_tensor_scan(tend[:, :], ntile[:, :], ntile[:, :], 0.0, ALU.add, ALU.bypass))
                link(nc.vector.tensor_tensor(base[:, :], tend[:, :], ntile[:, :], ALU.subtract))
                link(nc.vector.tensor_scalar(base[:, :], base[:, :], float(P), None, ALU.mult))
                link(nc.vector.tensor_tensor(base[:, :], base[:, :], cum[:, :, NT - 1], ALU.subtract))
                link(nc.vector.tensor_tensor(base[:, :], base[:, :], tot[:, :], ALU.add))
                link(nc.vector.tensor_tensor(slot[:, :, :], cum[:, :, :], cnt[:, :, :], ALU.subtract))
                link(nc.vector.tensor_tensor(slot[:, :, :], slot[:, :, :],
                                             base[:, :, None].to_broadcast([P, NE, NT]), ALU.add))
                link(nc.vector.tensor_tensor(slot[:, :, :], slot[:, :, :],
                                             bank[1][:, 0:NE * NT].rearrange("p (e j) -> p e j", e=NE), ALU.add))
                link(nc.vector.tensor_tensor(slot[:, :, :], slot[:, :, :], onehot[:, :, :], ALU.mult))
                link(nc.vector.tensor_reduce(posf[:, :], slot[:, :, :].rearrange("p e j -> p j e"), X, ALU.add))
                nc.vector.tensor_copy(pos[:, :], posf[:, :])
                link(nc.vector.tensor_tensor(big[:, :, :], slot_tile[:, :, None].to_broadcast([P, SLOT_TILES, NE]),
                                             tend[:, None, :].to_broadcast([P, SLOT_TILES, NE]), ALU.is_ge))
                link(nc.vector.tensor_reduce(exf[:, :], big[:, :, :], X, ALU.add))
                link(nc.vector.tensor_scalar(exf[:, :], exf[:, :], float(NE - 1), None, ALU.min))
                link(nc.vector.tensor_copy(guoff[:, :], exf[:, :]))

        with ExitStack() as ph:
            def sb3(name, shape, dt=fp32):
                return ph.enter_context(nc.sbuf_tensor(name, shape, dt))
            q_w = sb3("q_w", [P, L])
            k_w = sb3("k_w", [P, L])
            T2 = sb3("T2", [P, 2, L])
            T1 = sb3("T1", [P, 2, L])
            U = sb3("U", [P, L])
            W = sb3("W", [P, 2, L])
            PR = sb3("PR", [P, 2, L])
            PT = sb3("PT", [P, 2, TPB, P])
            wmax = sb3("wmax", [P, TPB])
            nbias = sb3("nbias", [P, TPB])
            rsum = sb3("rsum", [P, TPB])
            rinv = sb3("rinv", [P, TPB])
            sht = sb3("sht", [P, L])
            sha = sb3("sha", [P, L])
            shh = sb3("shh", [P, KI, L])
            xs_w = sb3("xs_w", [P, 2, TPB, D])
            pos_w = sb3("pos_w", [P, 2, TPB], u32)
            names = {"q_ps": 1, "k_ps": 1, "q_sb": 1, "k_sb": 1, "s_ps": TPB, "t2": TPB, "t1": TPB, "u": TPB,
                     "w": TPB, "mx": TPB, "nb": TPB, "p": TPB, "pT_ps": TPB, "pT_sb": TPB, "o_ps": TPB,
                     "rinv": 1, "attn": 1, "shg_ps": KI, "sht": KI, "sha": KI, "shh": KI, "shd_ps": 1, "res": 1}
            S = {n: sem("p3_" + n) for n in names}
            s_xs = [sem(f"p3_xs_ready_{i}") for i in range(2)]
            s_pw = [sem(f"p3_pos_ready_{i}") for i in range(2)]
            s_sc = [sem(f"p3_scattered_{i}") for i in range(2)]
            s_cr = sem("p3_credits_given")

            def at(b, n, c):
                return (b + 1) * names[n] + c

            block = ph.enter_context(nc.Block())

            @block.gpsimd
            def _(pool):
                for n, per in names.items():
                    pool.sem_inc(S[n], per)
                with pool.Fori(0, NB // 2) as b2:
                    for i in range(2):
                        nc.gpsimd.tensor_copy(pos_w[:, i, :], pos[:, ds((b2 * 2 + i) * TPB, TPB)]).then_inc(s_pw[i], 1)
                        nc.gpsimd.tensor_tensor(xs_w[:, i, :, :], nf_all[:, ds((b2 * 2 + i) * TPB, TPB), :],
                                                score[:, ds((b2 * 2 + i) * TPB, TPB), None]
                                                .to_broadcast([P, TPB, D]), ALU.mult).then_inc(s_xs[i], 1)
                        pool.wait_ge(s_pw[i], b2 + 1)
                        pool.wait_ge(s_xs[i], b2 + 1)
                        alone(pool)
                        for j in range(TPB):
                            pool.indirect_dma_start(
                                xs_dram, bass.IndirectOffsetOnAxis(ap=pos_w[:, i, j:j + 1], axis=0),
                                xs_w[:, i, j, :], None).then_inc(s_sc[i], 16)
                    for i in range(2):
                        pool.wait_ge(s_sc[i], (b2 + 1) * 16 * TPB)

            @block.tensor
            def _(pe):
                def queries_keys(b):
                    pe.wait_ge(S["shh"], at(b, "shh", 0))
                    nc.tensor.matmul(bank[5], WqT[:, :], xnT_all[:, ds(b * L, L)], start=True, stop=True)\
                        .then_inc(S["q_ps"], 1)
                    nc.tensor.matmul(bank[6], WkT[:, :], xnT_all[:, ds(b * L, L)], start=True, stop=True)\
                        .then_inc(S["k_ps"], 1)

                def scores(b, j):
                    if j == 0:
                        pe.wait_ge(S["q_sb"], at(b, "q_sb", 1))
                        pe.wait_ge(S["k_sb"], at(b, "k_sb", 1))
                    pe.wait_ge(S["u"], at(b, "u", j + 1 - 2))
                    nc.tensor.matmul(bank[j % 2], q_w[:, j * P:(j + 1) * P], k_w[:, :], start=True, stop=True)\
                        .then_inc(S["s_ps"], 1)

                def round_(b, more):
                    def w(n, c):
                        pe.wait_ge(S[n], at(b, n, c))

                    def shared_up(k):
                        w("shh", k)
                        nc.tensor.matmul(bank[5], shgu[:, k * P:(k + 1) * P], nfT_all[:, ds(b * L, L)],
                                         start=True, stop=True)
                        nc.tensor.matmul(bank[6], shgu[:, I + k * P:I + (k + 1) * P], nfT_all[:, ds(b * L, L)],
                                         start=True, stop=True).then_inc(S["shg_ps"], 1)

                    def turn(j):
                        w("p", j + 1)
                        w("pT_sb", j + 1 - 2)
                        for c in range(TPB):
                            ins = nc.tensor.transpose(bank[2 + j % 2][:, c * P:(c + 1) * P],
                                                      PR[:, j % 2, c * P:(c + 1) * P], ident)
                        ins.then_inc(S["pT_ps"], 1)

                    def values(j):
                        w("pT_sb", j + 1)
                        if j == 0:
                            w("attn", 0)
                        for c in range(TPB):
                            ins = nc.tensor.matmul(bank[4][:, j * P:(j + 1) * P], PT[:, j % 2, c, :],
                                                   vo_all[:, ds(b * TPB + c, 1), :],
                                                   start=(c == 0), stop=(c == TPB - 1))
                        ins.then_inc(S["o_ps"], 1)

                    w("q_sb", 1)
                    w("k_sb", 1)
                    shared_up(0)
                    turn(0)
                    scores(b, 2)
                    values(0)
                    shared_up(1)
                    turn(1)
                    scores(b, 3)
                    values(1)
                    if more:
                        queries_keys(b + 1)
                    turn(2)
                    values(2)
                    w("shh", KI)
                    w("res", 0)
                    for j in range(TPB):
                        for k in range(KI):
                            ins = nc.tensor.matmul(bank[7][:, j * P:(j + 1) * P], shh[:, k, j * P:(j + 1) * P],
                                                   shdown[:, k, :], start=(k == 0), stop=(k == KI - 1))
                    ins.then_inc(S["shd_ps"], 1)
                    turn(3)
                    if more:
                        scores(b + 1, 0)
                        scores(b + 1, 1)
                    values(3)

                pe.wait_ge(s_we, 16 * 8)
                queries_keys(0)
                scores(0, 0)
                scores(0, 1)
                with pe.Fori(0, NB - 1) as b:
                    round_(b, True)
                round_(NB - 1, False)

            @block.scalar
            def _(act):
                def keys(b):
                    act.wait_ge(S["k_ps"], at(b, "k_ps", 1))
                    act.wait_ge(S["s_ps"], at(b, "s_ps", 0))
                    nc.scalar.activation(k_w[:, :], bank[6], ACT.Identity, bias=cols[:, 1:2]).then_inc(S["k_sb"], 1)

                def round_(b, more):
                    def w(n, c):
                        act.wait_ge(S[n], at(b, n, c))

                    def tanhs(j):
                        w("s_ps", j + 1)
                        w("u", j + 1 - 2)
                        nc.scalar.activation(T2[:, j % 2, :], bank[j % 2], ACT.Tanh, scale=0.5).then_inc(S["t2"], 1)
                        w("w", j + 1 - 2)
                        nc.scalar.activation(T1[:, j % 2, :], bank[j % 2], ACT.Tanh).then_inc(S["t1"], 1)

                    def probs(j):
                        w("nb", j + 1)
                        w("pT_ps", j + 1 - 2)
                        if j == 0:
                            w("rinv", 0)
                        nc.scalar.activation(PR[:, j % 2, :], W[:, j % 2, :], ACT.Exp, bias=nbias[:, j:j + 1],
                                             scale=0.1, accum_out=rsum[:, j:j + 1]).then_inc(S["p"], 1)

                    def turned(j):
                        w("pT_ps", j + 1)
                        w("o_ps", j + 1 - 2)
                        nc.scalar.activation(PT[:, j % 2, :, :], bank[2 + j % 2].rearrange("p (c s) -> p c s", s=P),
                                             ACT.Copy).then_inc(S["pT_sb"], 1)

                    def shared(k):
                        w("shg_ps", k + 1)
                        w("sha", k)
                        nc.scalar.activation(sht[:, :], bank[5], ACT.Tanh, scale=0.5).then_inc(S["sht"], 1)

                    tanhs(0)
                    tanhs(1)
                    probs(0)
                    shared(0)
                    turned(0)
                    tanhs(2)
                    probs(1)
                    shared(1)
                    turned(1)
                    tanhs(3)
                    probs(2)
                    if more:
                        keys(b + 1)
                    turned(2)
                    probs(3)
                    turned(3)

                keys(0)
                with act.Fori(0, NB - 1) as b:
                    round_(b, True)
                round_(NB - 1, False)

            @block.vector
            def _(dve):
                def attended(b):
                    dve.wait_ge(S["rinv"], at(b, "rinv", 1))
                    dve.wait_ge(S["o_ps"], at(b, "o_ps", TPB))
                    nc.vector.tensor_tensor(attn_all[:, ds(b * TPB, TPB), :],
                                            bank[4].rearrange("p (j d) -> p j d", d=D),
                                            rinv[:, :, None].to_broadcast([P, TPB, D]), ALU.mult).then_inc(S["attn"], 1)

                def queries(b):
                    dve.wait_ge(S["q_ps"], at(b, "q_ps", 1))
                    dve.wait_ge(S["s_ps"], at(b, "s_ps", 0))
                    nc.vector.tensor_scalar(q_w[:, :], bank[5], cols[:, 0:1], None, ALU.add).then_inc(S["q_sb"], 1)

                def round_(b, first, more):
                    def w(n, c):
                        dve.wait_ge(S[n], at(b, n, c))

                    def theta(j):
                        w("t2", j + 1)
                        w("t1", j + 1)
                        w("w", j)
                        nc.vector.scalar_tensor_tensor(U[:, :], bank[j % 2], 0.0, T2[:, j % 2, :], ALU.max, ALU.add)\
                            .then_inc(S["u"], 1)
                        w("u", j + 1)
                        w("p", j + 1 - 2)
                        w("mx", j + 1 - 2)
                        nc.vector.scalar_tensor_tensor(W[:, j % 2, :], T1[:, j % 2, :], 1.5, U[:, :],
                                                       ALU.mult, ALU.add).then_inc(S["w"], 1)
                        w("w", j + 1)
                        w("nb", j + 1 - TPB)
                        nc.vector.tensor_reduce(wmax[:, j:j + 1], W[:, j % 2, :], X, ALU.max).then_inc(S["mx"], 1)
                        w("mx", j + 1)
                        w("p", j + 1 - TPB)
                        nc.vector.tensor_scalar(nbias[:, j:j + 1], wmax[:, j:j + 1], -0.1, None, ALU.mult)\
                            .then_inc(S["nb"], 1)

                    def shared(k):
                        w("sht", k + 1)
                        w("shh", k)
                        nc.vector.scalar_tensor_tensor(sha[:, :], sht[:, :], 1.0, bank[5], ALU.add, ALU.mult)\
                            .then_inc(S["sha"], 1)
                        w("sha", k + 1)
                        w("shd_ps", 0)
                        nc.vector.scalar_tensor_tensor(shh[:, k, :], sha[:, :], 0.5, bank[6], ALU.mult, ALU.mult)\
                            .then_inc(S["shh"], 1)

                    theta(0)
                    if not first:
                        attended(b - 1)
                    theta(1)
                    shared(0)
                    theta(2)
                    shared(1)
                    theta(3)
                    if more:
                        queries(b + 1)
                    w("shd_ps", 1)
                    nc.vector.tensor_tensor(res_all[:, ds(b * TPB, TPB), :], res_all[:, ds(b * TPB, TPB), :],
                                            bank[7].rearrange("p (j d) -> p j d", d=D), ALU.add).then_inc(S["res"], 1)
                    w("p", TPB)
                    w("attn", 0)
                    nc.vector.reciprocal(rinv[:, :], rsum[:, :]).then_inc(S["rinv"], 1)

                queries(0)
                round_(0, True, True)
                with dve.Fori(1, NB - 1) as b:
                    round_(b, False, True)
                round_(NB - 1, False, False)
                attended(NB - 1)

        with ExitStack() as ph:
            def sb4(name, shape, dt=fp32):
                return ph.enter_context(nc.sbuf_tensor(name, shape, dt))
            UN = 4
            ROUNDS = SLOT_TILES // UN
            xs_t = sb4("xs_t", [P, UN, D])
            xT = sb4("xT", [P, 2, P])
            th = sb4("th", [P, 2, I])
            ha = sb4("ha", [P, I])
            hm = sb4("hm", [P, 2, I])
            hT = sb4("hT", [P, 2, KI, P])
            yt = sb4("yt", [P, UN, D])
            names = {n: UN for n in ("xT_ps", "xT", "gu_ps", "th", "ha", "hm", "hT_ps", "hT", "y_ps", "y")}
            S = {n: sem("p4_" + n) for n in names}
            s_in = [sem(f"p4_slots_loaded_{i}") for i in range(UN)]
            s_out = [sem(f"p4_slots_stored_{i}") for i in range(UN)]
            gu_flat = gu[:, :, :].rearrange("p e i -> p (e i)")
            down_flat = down[:, :, :, :].rearrange("p e k d -> p (e k d)")

            def at(r, n, c):
                return (r + 1) * names[n] + c

            def slots(dram, r, u):
                return dram[ds((r * UN + u) * P, P), :]

            block = ph.enter_context(nc.Block())

            @block.sync
            def _(sp):
                for u in range(UN):
                    sp.dma_start(xs_t[:, u, :], slots(xs_dram, 0, u)).then_inc(s_in[u], 16)
                kh = "(h p) a -> p h a"
                loads = [(W_in[:, :], t["W_in"]), (convw[:, :, :], t["conv_w"].rearrange(kh, p=P)),
                         (convb[:, :], t["conv_b"].rearrange("(h p) -> p h", p=P)),
                         (W_x[:, :, :], t["W_x"].rearrange(kh, p=P)),
                         (b_dt[:, :], t["b_dt"].rearrange("(h p) -> p h", p=P)),
                         (A[:, :, :], t["A_log"].rearrange(kh, p=P)),
                         (Dcol[:, :], t["D"].rearrange("(h p) -> p h", p=P)),
                         (W_out[:, :, :], t["W_out"].rearrange(kh, p=P)),
                         (W_dt[0:RDT, :], t["W_dt"]),
                         (wi[:, 0:HID], t["wg"]), (wi[:, HID:2 * HID], t["wu"]),
                         (wi[:, 2 * HID:3 * HID].rearrange("p (k d) -> p k d", d=D),
                          t["wd"].rearrange("(k p) d -> p k d", p=P))]
                with nc.allow_non_contiguous_dma("columns of small vectors"):
                    for dst, src in loads:
                        sp.dma_start(dst, src).then_inc(s_lw, 16)
                with sp.Fori(0, ROUNDS - 1) as r:
                    for u in range(UN):
                        sp.wait_ge(S["xT_ps"], at(r, "xT_ps", u + 1))
                        sp.dma_start(xs_t[:, u, :], slots(xs_dram, r + 1, u)).then_inc(s_in[u], 16)
                        sp.wait_ge(S["y"], at(r, "y", u + 1))
                        sp.dma_start(slots(ys_dram, r, u), yt[:, u, :]).then_inc(s_out[u], 16)
                for u in range(UN):
                    sp.wait_ge(S["y"], at(ROUNDS - 1, "y", u + 1))
                    sp.dma_start(slots(ys_dram, ROUNDS - 1, u), yt[:, u, :]).then_inc(s_out[u], 16)
                for u in range(UN):
                    sp.wait_ge(s_out[u], 16 * (ROUNDS + 1))

            @block.gpsimd
            def _(pool):
                for n, per in names.items():
                    pool.sem_inc(S[n], per)
                for u in range(UN):
                    pool.sem_inc(s_out[u], 16)

            @block.tensor
            def _(pe):
                def turn_x(r, u):
                    pe.wait_ge(s_in[u % UN], 16 * (r + u // UN + 1))
                    pe.wait_ge(S["xT"], at(r, "xT", u + 1 - 2))
                    nc.tensor.transpose(bank[u % 2][:, 0:P], xs_t[:, u % UN, :], ident).then_inc(S["xT_ps"], 1)

                expert = {}

                def load_expert(r, u):
                    expert[u] = pe.value_load(guoff[0:1, ds(r * UN + u, 1)], min_val=0, max_val=NE - 1)

                def up(r, u):
                    e = expert[u]
                    pe.wait_ge(S["xT"], at(r, "xT", u + 1))
                    pe.wait_ge(S["hm"], at(r, "hm", u + 1 - 2))
                    alone(pe)
                    nc.tensor.matmul(bank[2 + u % 2], xT[:, u % 2, :], gu_flat[:, ds(e * (2 * I), 2 * I)],
                                     start=True, stop=True).then_inc(S["gu_ps"], 1)

                def turn_h(r, u):
                    pe.wait_ge(S["hm"], at(r, "hm", u + 1))
                    pe.wait_ge(S["hT"], at(r, "hT", u + 1 - 2))
                    for k in range(KI):
                        ins = nc.tensor.transpose(bank[4 + u % 2][:, k * P:(k + 1) * P],
                                                  hm[:, u % 2, k * P:(k + 1) * P], ident)
                    ins.then_inc(S["hT_ps"], 1)

                def dn(r, u):
                    pe.wait_ge(S["hT"], at(r, "hT", u + 1))
                    pe.wait_ge(S["y"], at(r, "y", u + 1 - 2))
                    alone(pe)
                    e = expert[u]
                    for k in range(KI):
                        ins = nc.tensor.matmul(bank[6 + u % 2][:, 0:D], hT[:, u % 2, k, :],
                                               down_flat[:, ds(e * (KI * D) + k * D, D)],
                                               start=(k == 0), stop=(k == KI - 1))
                    ins.then_inc(S["y_ps"], 1)

                def steps(r, first, last):
                    expert.clear()
                    load_expert(r, 1)
                    if not first:
                        load_expert(r, -1)
                    for u in range(UN):
                        if not (last and u == UN - 1):
                            up(r, u + 1)
                        if not (last and u >= UN - 2):
                            turn_x(r, u + 2)
                        if u == 1:
                            load_expert(r, 0)
                        if not (first and u == 0):
                            dn(r, u - 1)
                        if not (last and u >= UN - 2) and u < UN - 1:
                            load_expert(r, u + 2)
                        turn_h(r, u)

                turn_x(0, 0)
                turn_x(0, 1)
                load_expert(0, 0)
                up(0, 0)
                steps(0, True, False)
                with pe.Fori(1, ROUNDS - 1) as r:
                    steps(r, False, False)
                steps(ROUNDS - 1, False, True)
                dn(ROUNDS - 1, UN - 1)

            @block.scalar
            def _(act):
                def x_out(r, u):
                    act.wait_ge(S["xT_ps"], at(r, "xT_ps", u + 1))
                    act.wait_ge(S["gu_ps"], at(r, "gu_ps", u + 1 - 2))
                    nc.scalar.activation(xT[:, u % 2, :], bank[u % 2][:, 0:P], ACT.Copy).then_inc(S["xT"], 1)

                def tanh(r, u):
                    act.wait_ge(S["gu_ps"], at(r, "gu_ps", u + 1))
                    act.wait_ge(S["ha"], at(r, "ha", u + 1 - 2))
                    nc.scalar.activation(th[:, u % 2, :], bank[2 + u % 2][:, 0:I], ACT.Tanh, scale=0.5)\
                        .then_inc(S["th"], 1)

                x_out(0, 0)
                x_out(0, 1)
                with act.Fori(0, ROUNDS - 1) as r:
                    for u in range(UN):
                        tanh(r, u)
                        x_out(r, u + 2)
                for u in range(UN):
                    tanh(ROUNDS - 1, u)
                    if u + 2 < UN:
                        x_out(ROUNDS - 1, u + 2)

            @block.vector
            def _(dve):
                def hidden(r, u):
                    dve.wait_ge(S["th"], at(r, "th", u + 1))
                    dve.wait_ge(S["hm"], at(r, "hm", u))
                    nc.vector.scalar_tensor_tensor(ha[:, :], th[:, u % 2, :], 1.0, bank[2 + u % 2][:, 0:I],
                                                   ALU.add, ALU.mult).then_inc(S["ha"], 1)
                    dve.wait_ge(S["ha"], at(r, "ha", u + 1))
                    dve.wait_ge(S["hT_ps"], at(r, "hT_ps", u + 1 - 2))
                    nc.vector.scalar_tensor_tensor(hm[:, u % 2, :], ha[:, :], 0.5, bank[2 + u % 2][:, I:2 * I],
                                                   ALU.mult, ALU.mult).then_inc(S["hm"], 1)

                def h_out(r, u):
                    dve.wait_ge(S["hT_ps"], at(r, "hT_ps", u + 1))
                    dve.wait_ge(S["y_ps"], at(r, "y_ps", u + 1 - 2))
                    nc.vector.tensor_copy(hT[:, u % 2, :, :],
                                          bank[4 + u % 2][:, 0:KI * P].rearrange("p (k s) -> p k s", s=P))\
                        .then_inc(S["hT"], 1)

                def y_out(r, u):
                    dve.wait_ge(S["y_ps"], at(r, "y_ps", u + 1))
                    dve.wait_ge(s_out[u % UN], 16 * (r + 1 + (u - u % UN) // UN))
                    nc.vector.tensor_copy(yt[:, u % UN, :], bank[6 + u % 2][:, 0:D]).then_inc(S["y"], 1)

                def steps(r, first):
                    for u in range(UN):
                        hidden(r, u)
                        if not (first and u == 0):
                            y_out(r, u - 1)
                        h_out(r, u)

                steps(0, True)
                with dve.Fori(1, ROUNDS) as r:
                    steps(r, False)
                y_out(ROUNDS - 1, UN - 1)

        with ExitStack() as ph:
            def sb5(name, shape, dt=fp32):
                return ph.enter_context(nc.sbuf_tensor(name, shape, dt))
            NQ = 2 * TPB
            moe_w = sb5("moe_w", [P, 2, TPB, D])
            pos_w = sb5("pos_w5", [P, 2, TPB], u32)
            gp = sb5("gp", [P, 2, TPB * D])
            gt = sb5("gt", [P, 2, TPB * D])
            gg = sb5("gg", [P, TPB * D])
            sg = sb5("sg", [P, TPB * D])
            st_w = sb5("st_w", [P, NQ, 6])
            mean1 = sb5("mean1", [P, NQ])
            var1 = sb5("var1", [P, NQ])
            tmp1 = sb5("tmp1", [P, NQ])
            std1 = sb5("std1", [P, NQ])
            rs1 = sb5("rs1", [P, NQ])
            xn1 = sb5("xn1", [P, 2, TPB, D])
            s_pw = [sem(f"p5_pos_ready_{i}") for i in range(2)]
            s_moe = [sem(f"p5_gathered_{i}") for i in range(2)]
            s_amin = sem("p5_A_bounded")
            s_aexp = sem("p5_A_exp")
            names = {n: 2 for n in ("gp", "gt", "gg", "sg", "x1", "xn", "xT_ps", "xT")}
            names |= {"bn": 1, "mv": 7, "var": 1, "std": 1, "rs": 1}
            S = {n: sem("p5_" + n) for n in names}

            def at(r, n, c):
                return (r + 1) * names[n] + c

            block = ph.enter_context(nc.Block())

            @block.gpsimd
            def _(pool):
                for n, per in names.items():
                    pool.sem_inc(S[n], per)
                with pool.Fori(0, NB // 2) as r:
                    for i in range(2):
                        pool.wait_ge(S["gp"], at(r, "gp", i + 1 - 2))
                        nc.gpsimd.tensor_copy(pos_w[:, i, :], pos[:, ds((r * 2 + i) * TPB, TPB)]).then_inc(s_pw[i], 1)
                        pool.wait_ge(s_pw[i], r + 1)
                        alone(pool)
                        for j in range(TPB):
                            pool.indirect_dma_start(
                                moe_w[:, i, j, :], None, ys_dram,
                                bass.IndirectOffsetOnAxis(ap=pos_w[:, i, j:j + 1], axis=0)).then_inc(s_moe[i], 16)

            @block.tensor
            def _(pe):
                with pe.Fori(0, NB // 2) as r:
                    for i in range(2):
                        pe.wait_ge(S["xn"], at(r, "xn", i + 1))
                        pe.wait_ge(S["xT"], at(r, "xT", i + 1 - 2))
                        for j in range(TPB):
                            ins = nc.tensor.transpose(bank[i][:, j * P:(j + 1) * P], xn1[:, i, j, :], ident)
                        ins.then_inc(S["xT_ps"], 1)

            @block.scalar
            def _(act):
                act.wait_ge(s_amin, 1)
                nc.scalar.activation(A[:, :, :], A[:, :, :], ACT.Exp).then_inc(s_aexp, 1)

                def turned(r, i):
                    act.wait_ge(S["xT_ps"], at(r, "xT_ps", i + 1))
                    nc.scalar.activation(xn1T_all[:, ds((r * 2 + i) * L, L)], bank[i], ACT.Copy).then_inc(S["xT"], 1)

                def round_(r, first):
                    for i in range(2):
                        act.wait_ge(S["gp"], at(r, "gp", i + 1))
                        act.wait_ge(S["gg"], at(r, "gg", i + 1 - 2))
                        nc.scalar.activation(gt[:, i, :], gp[:, i, :], ACT.Tanh, scale=0.5).then_inc(S["gt"], 1)
                    if not first:
                        for i in range(2):
                            turned(r - 1, i)
                    act.wait_ge(S["var"], at(r, "var", 1))
                    act.wait_ge(S["rs"], at(r, "rs", 0))
                    nc.scalar.activation(std1[:, :], var1[:, :], ACT.Sqrt).then_inc(S["std"], 1)

                round_(0, True)
                with act.Fori(1, NB // 2) as r:
                    round_(r, False)
                for i in range(2):
                    turned(NB // 2 - 1, i)

            @block.vector
            def _(dve):
                dve.wait_ge(s_lw, 16 * 12)
                nc.vector.tensor_scalar(A[:, :, :], A[:, :, :], A_LOG_MAX, None, ALU.min).then_inc(s_amin, 1)
                nc.vector.tensor_scalar(convw[:, :, :], convw[:, :, :], 0.5, None, ALU.mult)
                nc.vector.tensor_scalar(convb[:, :], convb[:, :], 0.5, None, ALU.mult)
                for h in range(KH):
                    nc.vector.tensor_scalar(W_outD[:, h, :], W_out[:, h, :], Dcol[:, h:h + 1], None, ALU.mult)
                nc.vector.tensor_scalar(wgu[:, :], wi[:, 0:2 * HID], DEQUANT, None, ALU.mult)
                nc.vector.tensor_scalar(wd[:, :, :].rearrange("p k d -> p (k d)"), wi[:, 2 * HID:3 * HID],
                                        0.5 * DEQUANT, None, ALU.mult)
                dve.wait_ge(s_aexp, 1)
                nc.vector.tensor_scalar(A[:, :, :], A[:, :, :], -1.0, None, ALU.mult)

                def tok(a):
                    return a.rearrange("p (j d) -> p j d", d=D)

                def rng(a, r, i):
                    return a[:, ds((r * 2 + i) * TPB, TPB), :]

                def gate_in(r, i):
                    dve.wait_ge(s_moe[i], (r + 1) * 16 * TPB)
                    dve.wait_ge(S["gg"], at(r, "gg", i + 1 - 2))
                    nc.vector.tensor_tensor(tok(gp[:, i, :]), rng(res_all, r, i), moe_w[:, i, :, :], ALU.add)\
                        .then_inc(S["gp"], 1)

                def norm(r):
                    dve.wait_ge(S["std"], at(r, "std", 1))
                    nc.vector.reciprocal(rs1[:, :], std1[:, :]).then_inc(S["rs"], 1)
                    dve.wait_ge(S["rs"], at(r, "rs", 1))
                    for i in range(2):
                        dve.wait_ge(S["xT_ps"], at(r, "xT_ps", i + 1 - 2))
                        for j in range(TPB):
                            c = i * TPB + j
                            ins = nc.vector.tensor_scalar(xn1[:, i, j, :], x_all[:, ds(r * NQ + c, 1), :],
                                                          mean1[:, c:c + 1], rs1[:, c:c + 1], ALU.subtract, ALU.mult)
                        ins.then_inc(S["xn"], 1)

                def residual(r, i):
                    dve.wait_ge(S["gt"], at(r, "gt", i + 1))
                    dve.wait_ge(S["sg"], at(r, "sg", i))
                    nc.vector.scalar_tensor_tensor(gg[:, :], gt[:, i, :], 1.0, gp[:, i, :], ALU.add, ALU.mult)\
                        .then_inc(S["gg"], 1)
                    dve.wait_ge(S["gg"], at(r, "gg", i + 1))
                    dve.wait_ge(S["x1"], at(r, "x1", i))
                    nc.vector.scalar_tensor_tensor(tok(sg[:, :]), tok(gg[:, :]), 0.5, rng(attn_all, r, i),
                                                   ALU.mult, ALU.mult).then_inc(S["sg"], 1)
                    dve.wait_ge(S["sg"], at(r, "sg", i + 1))
                    nc.vector.tensor_tensor(rng(x_all, r, i), rng(x_all, r, i), tok(sg[:, :]), ALU.add)\
                        .then_inc(S["x1"], 1)

                def moments(r):
                    dve.wait_ge(S["x1"], at(r, "x1", 2))
                    dve.wait_ge(S["var"], at(r, "var", 0))
                    for c in range(NQ):
                        ins = nc.vector.bn_stats(st_w[:, c:c + 1, :], x_all[:, ds(r * NQ + c, 1), :])
                    ins.then_inc(S["bn"], 1)
                    dve.wait_ge(S["bn"], at(r, "bn", 1))
                    dve.wait_ge(S["xn"], at(r, "xn", 0))
                    dve.wait_ge(S["std"], at(r, "std", 0))
                    n = [0]

                    def link(ins):
                        n[0] += 1
                        ins.then_inc(S["mv"], 1)
                        dve.wait_ge(S["mv"], at(r, "mv", n[0]))

                    mean_var(dve, link, mean1[:, :], var1[:, :], tmp1[:, :], st_w)
                    nc.vector.tensor_scalar(var1[:, :], var1[:, :], LN_EPS, None, ALU.add).then_inc(S["var"], 1)

                def round_(r, first):
                    gate_in(r, 0)
                    if not first:
                        norm(r - 1)
                    residual(r, 0)
                    gate_in(r, 1)
                    residual(r, 1)
                    moments(r)

                round_(0, True)
                with dve.Fori(1, NB // 2) as r:
                    round_(r, False)
                norm(NB // 2 - 1)

        layer0.close()
        with ExitStack() as ph:
            def sb6(name, shape, dt=fp32):
                return ph.enter_context(nc.sbuf_tensor(name, shape, dt))
            NP = NS // 2
            RB = RDT + NS
            R = 4
            Bbc = attn_all[:, :, :].rearrange("p j d -> p (j d)").rearrange("p (n l) -> p n l", l=L)
            Bbc2 = nf_all[:, :, :].rearrange("p j d -> p (j d)").rearrange("p (n l) -> p n l", l=L)

            def B_pair(q):
                half = Bbc if q < NP // 2 else Bbc2
                m = (2 * q) % (NS // 2)
                return half[:, m:m + 2, :]
            hring = xnT_all[:, :].rearrange("p (r n l) -> p r n l", n=2, l=L)
            dbx = nfT_all[:, :].rearrange("p (r n l) -> p r n l", n=2, l=L)
            dA = res_all[:, :, :].rearrange("p j d -> p (j d)").rearrange("p (r n l) -> p r n l", n=2, l=L)

            cbuf = sb6("cbuf", [P, KH, TAPS - 1 + L])
            yh = sb6("yh", [P, KH, L])
            tc_ = sb6("tconv", [P, KH, L])
            xv = sb6("xv", [P, KH, L])
            tf = sb6("tf", [P, L])
            fa = sb6("fa", [P, L])
            hff = sb6("hff", [P, KF, L])
            ssmT = sb6("ssmT", [P, L])
            Cc = sb6("Cc", [P, 2, TPB, NS])
            tg = sb6("tg", [P, L])
            G1 = sb6("G1", [P, 2, L])
            ab = sb6("ab", [P, KH, L])
            rl = sb6("rl", [P, KH, L])
            lg = sb6("lg", [P, KH, L])
            e1 = sb6("e1", [P, KH, L])
            delta = sb6("delta", [P, 2, KH, L])
            du = sb6("du", [P, 2, KH, L])
            acc = sb6("acc", [P, 2, TPB, D])
            ow = sb6("ow", [P, TPB, D])
            og = sb6("og", [P, TPB, D])
            s_set = sem("p6_zeros_set")
            s_bst = sem("p6_B_stored")
            s_bld = [sem(f"p6_B_loaded_{q}") for q in range(NP)]
            s_o = sem("p6_out_stored")
            names = {"xv_ps": KH, "cb": KH, "tap0": KH, "tap": KH * (TAPS - 2), "yh": KH,
                     "tc": KH, "xv": KH, "ff_ps": KF, "tf": KF, "fa": KF, "hf": KF, "ssm_ps": 1, "ssm": 1,
                     "C_ps": 1, "C": 1, "dn_ps": 1, "tg": 1, "G1": 1, "dt_ps": KH, "rl": KH, "ey": 1, "lg": 1,
                     "e1": 1, "corr": 1, "sp": 1, "delta": 1, "du": 1, "acc_ps": 1, "acc0": 1,
                     "dA": 2 * NP, "dbx": 2 * NP, "scan": 2 * NP, "G": NS, "acc": NS * TPB, "og": 1, "ow": 1}
            S = {n: sem("p6_" + n) for n in names}

            def at(b, n, c):
                return (b + 2) * names[n] + c

            bF, bD, bK, Gb, bP = (0, 1), 2, 3, (4, 5), (6, 7)

            def rounds(eng, round_):
                round_(-1, 1, scan=False, prep=True, end=False)
                round_(0, 0, scan=True, prep=True, end=False)
                with eng.Fori(0, (NB - 2) // 2) as r:
                    round_(r * 2 + 1, 1, scan=True, prep=True, end=True)
                    round_(r * 2 + 2, 0, scan=True, prep=True, end=True)
                round_(NB - 1, 1, scan=True, prep=False, end=True)
                round_(NB, 0, scan=False, prep=False, end=True)

            block = ph.enter_context(nc.Block())

            @block.sync
            def _(sp):
                def round_(b, p, scan, prep, end):
                    if end:
                        sp.wait_ge(S["ow"], at(b - 1, "ow", 1))
                        alone(sp)
                        sp.dma_start(out[ds(b - 1, 1)].rearrange("a (j p) d -> p (a j) d", p=P), ow[:, :, :])\
                            .then_inc(s_o, 16)
                    if prep:
                        sp.wait_ge(S["ssm"], at(b + 1, "ssm", 1))
                        alone(sp)
                        sp.dma_start(bt_dram[ds(b + 1, 1)].rearrange("a n l -> (a n) l"), ssmT[RDT:RDT + NS, :])\
                            .then_inc(s_bst, 16)
                        sp.wait_ge(s_bst, (b + 3) * 16)
                        alone(sp)
                        for q in range(NP):
                            sp.wait_ge(S["dbx"], at(b, "dbx", 2 * q + 2))
                            alone(sp)
                            sp.dma_start(B_pair(q), bt_dram[ds(b + 1, 1), 2 * q:2 * q + 2, :].to_broadcast([P, 2, L]))\
                                .then_inc(s_bld[q], 16)

                rounds(sp, round_)
                sp.wait_ge(s_o, 16 * (NB + 1))

            @block.gpsimd
            def _(pool):
                for n, per in names.items():
                    pool.sem_inc(S[n], 2 * per)
                pool.sem_inc(s_bst, 16)
                pool.sem_inc(s_o, 16)

                def round_(b, p, scan, prep, end):
                    def output():
                        pool.wait_ge(S["acc"], at(b - 1, "acc", NS * TPB))
                        pool.wait_ge(S["G1"], at(b - 1, "G1", 1))
                        pool.wait_ge(S["ow"], at(b - 1, "ow", 0))
                        nc.gpsimd.tensor_tensor(og[:, :, :], acc[:, 1 - p, :, :],
                                                G1[:, 1 - p, :].rearrange("p (j d) -> p j d", d=D),
                                                ALU.mult).then_inc(S["og"], 1)
                        pool.wait_ge(S["og"], at(b - 1, "og", 1))
                        pool.wait_ge(s_o, b * 16)
                        nc.gpsimd.tensor_tensor(ow[:, :, :], og[:, :, :], x_all[:, ds((b - 1) * TPB, TPB), :], ALU.add)\
                            .then_inc(S["ow"], 1)

                    if scan:
                        pool.wait_ge(S["delta"], at(b, "delta", 1))
                        pool.wait_ge(S["xv"], at(b, "xv", KH))
                        pool.wait_ge(S["dbx"], at(b - 1, "dbx", 0))
                        nc.gpsimd.tensor_tensor(du[:, p, :, :], delta[:, p, :, :], xv[:, :, :], ALU.mult)\
                            .then_inc(S["du"], 1)
                        pool.wait_ge(S["du"], at(b, "du", 1))
                        for q in range(NP):
                            if q == 3 and end:
                                output()
                            pool.wait_ge(s_bld[q], (b + 1) * 16)
                            for h in range(KH):
                                i = 2 * q + h
                                pool.wait_ge(S["scan"], at(b, "scan", i + 1 - R))
                                nc.gpsimd.tensor_tensor(dbx[:, i % R, :, :], B_pair(q),
                                                        du[:, p, h:h + 1, :].to_broadcast([P, 2, L]), ALU.mult)\
                                    .then_inc(S["dbx"], 1)
                    elif end:
                        output()

                rounds(pool, round_)

            @block.tensor
            def _(pe):
                def mm(o, l, r, start=True, stop=True):
                    return nc.tensor.matmul(o, l, r, start=start, stop=stop)

                def round_(b, p, scan, prep, end):
                    def w(n, c):
                        pe.wait_ge(S[n], at(b + 1, n, c))

                    def project(n):
                        if not scan:
                            return
                        q = n // 2
                        pe.wait_ge(S["scan"], at(b, "scan", 2 * q + 2))
                        pe.wait_ge(S["acc"], at(b, "acc", (n + 1 - 2) * TPB))
                        for j in range(TPB):
                            for h in range(KH):
                                ins = mm(bank[Gb[n % 2]][:, j * P:(j + 1) * P],
                                         hring[:, (2 * q + h) % R, n % 2, j * P:(j + 1) * P], W_out[:, h, :],
                                         h == 0, h == KH - 1)
                        ins.then_inc(S["G"], 1)

                    def x_in(h):
                        w("rl", h + 1 - KH)
                        mm(bank[bP[h]], W_in[:, h * P:(h + 1) * P], xn1T_all[:, ds((b + 1) * L, L)])\
                            .then_inc(S["xv_ps"], 1)

                    def ffn_up(k):
                        w("hf", k)
                        mm(bank[bF[0]], wgu[:, k * P:(k + 1) * P], xn1T_all[:, ds((b + 1) * L, L)])
                        mm(bank[bF[1]], wgu[:, HID + k * P:HID + (k + 1) * P], xn1T_all[:, ds((b + 1) * L, L)])\
                            .then_inc(S["ff_ps"], 1)

                    def ssm():
                        w("cb", KH)
                        w("tap0", KH)
                        w("xv", KH)
                        for h in range(KH):
                            ins = mm(bank[bP[0]][0:RB, :], W_x[:, h, 0:RB], xv[:, h, :], h == 0, h == KH - 1)
                        ins.then_inc(S["ssm_ps"], 1)

                    def C_rows():
                        for j in range(TPB):
                            for h in range(KH):
                                ins = mm(bank[bP[1]][:, j * NS:(j + 1) * NS], xv[:, h, j * P:(j + 1) * P],
                                         W_x[:, h, RDT + NS:RX], h == 0, h == KH - 1)
                        ins.then_inc(S["C_ps"], 1)

                    def dt(h):
                        w("ssm", 1)
                        if h:
                            w("C", 1)
                        mm(bank[bP[h]], W_dt[:, h * P:(h + 1) * P], ssmT[:, :]).then_inc(S["dt_ps"], 1)

                    def skip():
                        w("xv", KH)
                        w("acc0", 0)
                        for j in range(TPB):
                            for h in range(KH):
                                ins = mm(bank[bK][:, j * P:(j + 1) * P], xv[:, h, j * P:(j + 1) * P], W_outD[:, h, :],
                                         h == 0, h == KH - 1)
                        ins.then_inc(S["acc_ps"], 1)

                    def ffn_down():
                        w("hf", KF)
                        w("G1", 0)
                        for j in range(TPB):
                            for k in range(KF):
                                ins = mm(bank[bD][:, j * P:(j + 1) * P], hff[:, k, j * P:(j + 1) * P], wd[:, k, :],
                                         k == 0, k == KF - 1)
                        ins.then_inc(S["dn_ps"], 1)

                    if prep:
                        x_in(0)
                        x_in(1)
                        ffn_up(0)
                    project(0)
                    project(1)
                    project(2)
                    project(3)
                    if prep:
                        ssm()
                        C_rows()
                    project(4)
                    if prep:
                        dt(0)
                    project(5)
                    if prep:
                        dt(1)
                    project(6)
                    project(7)
                    if prep:
                        ffn_up(1)
                    project(8)
                    project(9)
                    if prep:
                        skip()
                    project(10)
                    project(11)
                    if prep:
                        ffn_up(2)
                    project(12)
                    project(13)
                    if prep:
                        ffn_down()
                    project(14)
                    project(15)

                pe.wait_ge(s_set, 1)
                rounds(pe, round_)

            @block.scalar
            def _(act):
                act.wait_ge(s_set, 1)

                def decays(b, p, q):
                    if q == 0:
                        act.wait_ge(S["delta"], at(b, "delta", 1))
                    for h in range(KH):
                        i = 2 * q + h
                        act.wait_ge(S["scan"], at(b, "scan", i + 1 - R))
                        for k in range(2):
                            ins = nc.scalar.activation(dA[:, i % R, k, 1:L], delta[:, p, h, 1:L], ACT.Exp,
                                                       scale=A[:, h, 2 * q + k:2 * q + k + 1])
                        ins.then_inc(S["dA"], 1)

                def round_(b, p, scan, prep, end):
                    def w(n, c):
                        act.wait_ge(S[n], at(b + 1, n, c))

                    def conv_in(h):
                        w("xv_ps", h + 1)
                        w("yh", h + 1 - KH)
                        nc.scalar.activation(cbuf[:, h, TAPS - 1:TAPS - 1 + L], bank[bP[h]], ACT.Copy)\
                            .then_inc(S["cb"], 1)
                        w("tc", h + 1 - KH)
                        w("xv", h + 1 - KH)
                        nc.scalar.activation(yh[:, h, :], bank[bP[h]], ACT.Identity, bias=convb[:, h:h + 1],
                                             scale=convw[:, h, TAPS - 1:TAPS]).then_inc(S["tap0"], 1)

                    def conv_tanh(h):
                        w("yh", h + 1)
                        w("xv", h + 1 - KH)
                        nc.scalar.activation(tc_[:, h, :], yh[:, h, :], ACT.Tanh).then_inc(S["tc"], 1)

                    def ffn_tanh(k):
                        w("ff_ps", k + 1)
                        w("fa", k)
                        nc.scalar.activation(tf[:, :], bank[bF[0]], ACT.Tanh, scale=0.5).then_inc(S["tf"], 1)

                    def ssm_out():
                        w("ssm_ps", 1)
                        w("dt_ps", 0)
                        act.wait_ge(s_bst, (b + 2) * 16)
                        nc.scalar.activation(ssmT[0:RB, :], bank[bP[0]][0:RB, :], ACT.Copy).then_inc(S["ssm"], 1)

                    def C_out():
                        w("C_ps", 1)
                        act.wait_ge(S["acc"], at(b, "acc", 0))
                        nc.scalar.activation(Cc[:, 1 - p, :, :],
                                             bank[bP[1]][:, 0:TPB * NS].rearrange("p (j n) -> p j n", n=NS), ACT.Copy)\
                            .then_inc(S["C"], 1)

                    def abs_relu(h):
                        w("dt_ps", h + 1)
                        w("corr", 0)
                        w("lg", 0)
                        w("delta", 0)
                        nc.scalar.activation(ab[:, h, :], bank[bP[h]], ACT.Abs, bias=b_dt[:, h:h + 1])
                        nc.scalar.activation(rl[:, h, :], bank[bP[h]], ACT.Relu, bias=b_dt[:, h:h + 1])\
                            .then_inc(S["rl"], 1)

                    def exp_ln():
                        w("rl", KH)
                        nc.scalar.activation(ab[:, :, :], ab[:, :, :], ACT.Exp, scale=-1.0).then_inc(S["ey"], 1)
                        w("ey", 1)
                        w("sp", 0)
                        nc.scalar.activation(lg[:, :, :], ab[:, :, :], ACT.Ln, bias=1.0).then_inc(S["lg"], 1)

                    def skip_out():
                        w("acc_ps", 1)
                        act.wait_ge(S["og"], at(b, "og", 0))
                        nc.scalar.activation(acc[:, 1 - p, :, :], bank[bK].rearrange("p (j d) -> p j d", d=D), ACT.Copy)\
                            .then_inc(S["acc0"], 1)

                    def gate_tanh():
                        w("dn_ps", 1)
                        w("G1", 0)
                        nc.scalar.activation(tg[:, :], bank[bD], ACT.Tanh).then_inc(S["tg"], 1)

                    if prep:
                        conv_in(0)
                        conv_in(1)
                        ffn_tanh(0)
                    if scan:
                        decays(b, p, 2)
                    if prep:
                        conv_tanh(0)
                        conv_tanh(1)
                    if scan:
                        decays(b, p, 3)
                        decays(b, p, 4)
                    if prep:
                        ssm_out()
                        C_out()
                        abs_relu(0)
                        abs_relu(1)
                        exp_ln()
                    if scan:
                        decays(b, p, 5)
                    if prep:
                        ffn_tanh(1)
                    if scan:
                        decays(b, p, 6)
                    if prep:
                        ffn_tanh(2)
                    if scan:
                        decays(b, p, 7)
                    if prep:
                        skip_out()
                        decays(b + 1, 1 - p, 0)
                        gate_tanh()
                        decays(b + 1, 1 - p, 1)

                rounds(act, round_)

            @block.vector
            def _(dve):
                nc.vector.memset(ssmT[:, :], 0.0)
                nc.vector.memset(cbuf[:, :, 0:TAPS - 1], 0.0)
                nc.vector.memset(dA[:, :, :, 0:1], 0.0).then_inc(s_set, 1)

                def round_(b, p, scan, prep, end):
                    def w(n, c):
                        dve.wait_ge(S[n], at(b + 1, n, c))

                    def ws(n, c):
                        dve.wait_ge(S[n], at(b, n, c))

                    def scans(q):
                        if not scan:
                            return
                        for h in range(KH):
                            i = 2 * q + h
                            ws("dA", i + 1)
                            ws("dbx", i + 1)
                            ws("G", 2 * (q + 1 - 2))
                            nc.vector.tensor_tensor_scan(hring[:, i % R, :, :].rearrange("p n l -> p (n l)"),
                                                         dA[:, i % R, :, :].rearrange("p n l -> p (n l)"),
                                                         dbx[:, i % R, :, :].rearrange("p n l -> p (n l)"),
                                                         0.0, ALU.mult, ALU.add).then_inc(S["scan"], 1)

                    def add_state(b, p, m):
                        dve.wait_ge(S["G"], at(b, "G", m + 1))
                        if m == 0:
                            dve.wait_ge(S["acc0"], at(b, "acc0", 1))
                            dve.wait_ge(S["C"], at(b, "C", 1))
                        for j in range(TPB):
                            if m:
                                dve.wait_ge(S["acc"], at(b, "acc", (m - 1) * TPB + j + 1))
                            nc.vector.scalar_tensor_tensor(acc[:, p, j, :], bank[Gb[m % 2]][:, j * P:(j + 1) * P],
                                                           Cc[:, p, j, m:m + 1], acc[:, p, j, :],
                                                           ALU.mult, ALU.add).then_inc(S["acc"], 1)

                    def conv(h):
                        w("cb", h + 1)
                        w("tap0", h + 1)
                        for k in range(TAPS - 1):
                            if k:
                                w("tap", h * (TAPS - 2) + k)
                            ins = nc.vector.scalar_tensor_tensor(yh[:, h, :], cbuf[:, h, k:k + L],
                                                                 convw[:, h, k:k + 1], yh[:, h, :],
                                                                 ALU.mult, ALU.add)
                            ins.then_inc(S["tap" if k < TAPS - 2 else "yh"], 1)

                    def conv_silu():
                        w("acc_ps", 0)
                        w("du", 0)
                        for h in range(KH):
                            w("tc", h + 1)
                            nc.vector.scalar_tensor_tensor(xv[:, h, :], tc_[:, h, :], 1.0, yh[:, h, :],
                                                           ALU.add, ALU.mult).then_inc(S["xv"], 1)

                    def ffn_hidden(k):
                        w("tf", k + 1)
                        w("hf", k)
                        nc.vector.scalar_tensor_tensor(fa[:, :], tf[:, :], 1.0, bank[bF[0]], ALU.add, ALU.mult)\
                            .then_inc(S["fa"], 1)
                        w("fa", k + 1)
                        w("dn_ps", 0)
                        nc.vector.scalar_tensor_tensor(hff[:, k, :], fa[:, :], 0.5, bank[bF[1]], ALU.mult, ALU.mult)\
                            .then_inc(S["hf"], 1)

                    def softplus_low():
                        w("ey", 1)
                        w("delta", 0)
                        nc.vector.tensor_scalar(e1[:, :, :], ab[:, :, :], 1.0, 1.0, ALU.add, ALU.subtract)\
                            .then_inc(S["e1"], 1)
                        w("e1", 1)
                        nc.vector.tensor_tensor(e1[:, :, :], ab[:, :, :], e1[:, :, :], ALU.subtract)\
                            .then_inc(S["corr"], 1)

                    def softplus_sum():
                        w("corr", 1)
                        w("lg", 1)
                        nc.vector.tensor_tensor(e1[:, :, :], e1[:, :, :], lg[:, :, :], ALU.add).then_inc(S["sp"], 1)
                        w("sp", 1)
                        w("rl", KH)
                        dve.wait_ge(S["dA"], at(b, "dA", 0))
                        dve.wait_ge(S["du"], at(b, "du", 0))
                        nc.vector.tensor_tensor(delta[:, 1 - p, :, :], e1[:, :, :], rl[:, :, :], ALU.add)\
                            .then_inc(S["delta"], 1)

                    def gate():
                        ws("tg", 1)
                        dve.wait_ge(S["og"], at(b - 1, "og", 0))
                        nc.vector.scalar_tensor_tensor(G1[:, p, :], tg[:, :], 1.0, bank[bD], ALU.add, ALU.mult)\
                            .then_inc(S["G1"], 1)

                    for q in range(NP):
                        scans(q)
                        if q == 0:
                            if end:
                                add_state(b - 1, 1 - p, NS - 2)
                                add_state(b - 1, 1 - p, NS - 1)
                        elif scan:
                            add_state(b, p, 2 * q - 2)
                            add_state(b, p, 2 * q - 1)
                            if q == 1:
                                gate()
                        if not prep:
                            continue
                        if q == 0:
                            conv(0)
                            conv(1)
                        elif q == 1:
                            conv_silu()
                        elif q == 2:
                            ffn_hidden(0)
                        elif q == 4:
                            softplus_low()
                        elif q == 5:
                            softplus_sum()
                            ffn_hidden(1)
                        elif q == 6:
                            ffn_hidden(2)

                rounds(dve, round_)


_RENAME = {"x": "L0_attn_x", "Wv": "L0_attn_Wv", "bq": "L0_attn_bq", "bk": "L0_attn_bk", "bv": "L0_attn_bv",
           "bo": "L0_attn_bo", "ln_w": "L0_ffn_ln_w", "ln_b": "L0_ffn_ln_b", "router": "L0_ffn_router_w",
           "gate": "L0_ffn_gate_w", "up": "L0_ffn_up_w", "down": "L0_ffn_down_w", "sh_gate": "L0_ffn_sh_gate",
           "sh_up": "L0_ffn_sh_up", "sh_down": "L0_ffn_sh_down", "W_in": "L1_attn_W_in", "conv_b": "L1_attn_conv_b",
           "W_x": "L1_attn_W_x", "W_dt": "L1_attn_W_dt", "b_dt": "L1_attn_b_dt", "A_log": "L1_attn_A_log",
           "D": "L1_attn_D", "W_out": "L1_attn_W_out"}
_TRANSPOSED = {"WqT": "L0_attn_Wq", "WkT": "L0_attn_Wk", "WoT": "L0_attn_Wo", "wg": "L1_ffn_w_gate",
               "wu": "L1_ffn_w_up", "wd": "L1_ffn_w_down"}


def _shape_constants(tiles, experts):
    import numpy as np
    p = np.arange(128)
    over = np.ones((128, 1), np.float32)
    parts = [np.eye(128), (p[:, None] < p[None, :]), np.ones((128, 128)), over * (128 * np.arange(tiles)),
             over * np.arange(tiles + experts), over * (np.arange(experts) - experts)]
    return np.ascontiguousarray(np.concatenate([a.astype(np.float32) for a in parts], axis=1))


def kernel(**inputs):
    import numpy as _np
    import concourse.bacc as _bacc
    from concourse import mybir as _mybir
    from concourse.bass_utils import run_bass_kernel_spmd as _run

    arrays = {n: _np.ascontiguousarray(inputs[m]) for n, m in _RENAME.items()}
    arrays |= {n: _np.ascontiguousarray(_np.asarray(inputs[m]).T) for n, m in _TRANSPOSED.items()}
    arrays["conv_w"] = _np.ascontiguousarray(_np.asarray(inputs["L1_attn_conv_w"])[:, 0, :])
    nb, length, d = arrays["x"].shape
    arrays["const"] = _shape_constants(nb * length // 128, arrays["router"].shape[1])
    nc = _bacc.Bacc("TRN2", target_bir_lowering=False, num_devices=1)
    t = {n: nc.dram_tensor(f"in_{n}_dram", a.shape, _mybir.dt.from_np(a.dtype), kind="ExternalInput").ap()
         for n, a in arrays.items()}
    out = nc.dram_tensor("out_dram", (nb, length, d), _mybir.dt.float32, kind="ExternalOutput").ap()
    attention_moe_mamba_ffn(nc, t, out)
    r = _run(nc, [{f"in_{n}_dram": a for n, a in arrays.items()}], core_ids=[0])
    return r.results[0]["out_dram"]
```
